# Optimizing a Trainium2 kernel written in Bass

```python
import numpy as np
import jax
import jax.numpy as jnp

def _softmax(x, axis=-1):
    return jax.nn.softmax(x, axis=axis)

def _gelu(x):
    return jax.nn.gelu(x, approximate=True)

def _silu(x):
    return jax.nn.silu(x)

def _sigmoid(x):
    return jax.nn.sigmoid(x)

def _layernorm(x, axis=-1, eps=1e-05):
    m = jnp.mean(x, axis=axis, keepdims=True)
    v = jnp.var(x, axis=axis, keepdims=True)
    return (x - m) / jnp.sqrt(v + eps)

def _scatter_add(tgt, idx, src, axis=0):
    return tgt.at[idx].add(src)

def _segment_sum(src, seg, n):
    return jax.ops.segment_sum(src, seg, n)
kernel_name = 'mk_gnn_resnorm_d1_gnn_r8_04a72b'

def setup_inputs(seed: int=0):
    np.random.seed(seed)
    _w = jnp.asarray

    def _rec_inputs():
        import jax
        import jax.numpy as jnp
        _gk = jax.random.key(seed)
        x = -0.0008691 + 1 * jax.random.normal(jax.random.fold_in(_gk, 1), (6250, 128), jnp.float32)
        _s = jax.random.randint(jax.random.fold_in(_gk, 2), (100000,), 0, 6250, jnp.int32)
        _d = jax.random.randint(jax.random.fold_in(_gk, 3), (100000,), 0, 6250, jnp.int32)
        _loop = jnp.arange(6250, dtype=jnp.int32)
        src = jnp.concatenate([_s, _d, _loop])
        dst = jnp.concatenate([_d, _s, _loop])
        _o = jnp.argsort(dst, stable=True)
        src = src[_o]
        dst = dst[_o]
        return (x, src, dst)
    x, src, dst = _rec_inputs()

    def _L0_gnn_setup():
        import jax, jax.numpy as jnp
        import numpy as np
        N_NODES = 1250
        N_EDGES = 80000
        IN_CH = 128
        OUT_CH = 128
        key = jax.random.key(seed)
        k1, k2, k3, k4 = jax.random.split(key, 4)
        x = jax.random.normal(k1, (N_NODES, IN_CH), dtype=jnp.float32)
        edge_index = jax.random.randint(k2, (2, N_EDGES), 0, N_NODES, dtype=jnp.int64)
        bound = 1.0 / np.sqrt(2 * IN_CH)
        W = jax.random.uniform(k3, (OUT_CH, 2 * IN_CH), dtype=jnp.float32, minval=-bound, maxval=bound)
        b = jax.random.uniform(k4, (OUT_CH,), dtype=jnp.float32, minval=-bound, maxval=bound)
        return {'x': x, 'W': W, 'b': b, 'edge_index': edge_index}
    _L0_gnn_all = _L0_gnn_setup()
    _L0_gnn_in = {k: v for k, v in _L0_gnn_all.items() if k in ('W', 'b')}
    del _L0_gnn_all
    return {'x': x, 'src': src, 'dst': dst, 'L0_gnn_W': _L0_gnn_in['W'], 'L0_gnn_b': _L0_gnn_in['b']}

def reference(x, src, dst, L0_gnn_W, L0_gnn_b):
    import jax
    import jax.numpy as jnp

    def _L0_gnn_ref(x, W, b, edge_index):
        import jax, jax.numpy as jnp
        import numpy as np
        N_NODES = 1250
        N_EDGES = 80000
        IN_CH = 128
        OUT_CH = 128
        src, dst = (edge_index[0], edge_index[1])
        x_i = x[dst]
        x_j = x[src]
        feat = jnp.concatenate([x_i, x_j - x_i], axis=-1)
        msg = feat @ W.T + b
        out = jax.ops.segment_max(msg, dst, num_segments=x.shape[0])
        return jnp.where(jnp.isfinite(out), out, 0.0)
    edge_index = jnp.stack([src, dst])
    x = _layernorm(x + _L0_gnn_ref(x, L0_gnn_W, L0_gnn_b, edge_index), axis=-1)
    return x

_drawn_inputs = setup_inputs


def setup_inputs(seed=0):
    import zlib

    import numpy as np

    out = dict(_drawn_inputs(seed))
    spreads = {}
    factors = {}
    for name, (base, spread) in spreads.items():
        noise = np.random.default_rng([zlib.crc32(name.encode()), seed]).standard_normal(out[name].shape)
        drawn = base * np.exp(spread * noise) if base else spread * noise
        out[name] = jnp.asarray(drawn.astype(out[name].dtype))
    for name, factor in factors.items():
        out[name] = (out[name] * factor).astype(out[name].dtype)
    return out
```

```python
from contextlib import ExitStack

import concourse.bass as bass
from concourse import mybir

P = 128
F32 = mybir.dt.float32
BF16 = mybir.dt.bfloat16
I32 = mybir.dt.int32
ALU = mybir.AluOpType
ACT = mybir.ActivationFunctionType
AX_X = mybir.AxisListType.X

F32_MAX = 3.4028234663852886e38
ROUND = 12582912.0
FAR = float(1 << 20)
EPS = 1e-5


def largest_divisor(n, most):
    return max(d for d in range(1, most + 1) if n % d == 0)


def build(nc, x, src, dst, W, b, out):
    N, D = x.shape
    E, = src.shape
    HI = largest_divisor(N, P - 1)
    LO = N // HI
    EDGE_COLS = -(-E // P)
    LAST_COLS = E - (P - 1) * EDGE_COLS
    U = largest_divisor(EDGE_COLS // 2, 16)
    BLOCKS = EDGE_COLS // U
    PAIRS = BLOCKS // 2
    assert PAIRS * 2 * U == EDGE_COLS and 0 < LAST_COLS <= EDGE_COLS and D == P
    HISTORY_ROWS = P * EDGE_COLS
    GROUP = 4
    GROUPS = -(-LO // GROUP)
    CHUNK_GROUPS = [0, 2, 5, 8, 11, GROUPS]
    CHUNKS = len(CHUNK_GROUPS) - 1
    CHUNK_LO = [min(g * GROUP, LO) for g in CHUNK_GROUPS]
    OUT_LO = [0, 10, 20, 30, 38, 44, 48, LO]
    OUTS = len(OUT_LO) - 1
    OUT_W = max(OUT_LO[i + 1] - OUT_LO[i] for i in range(OUTS))
    HI_SPLIT = [(0, HI // 16 * 16), (HI // 16 * 16, HI)]
    EDGE_SPLIT = [(0, 112), (112, P - 1)]

    table = nc.dram_tensor("table", [N, D], F32, kind="Internal").ap()
    history = nc.dram_tensor("history", [HISTORY_ROWS + P, D], F32, kind="Internal").ap()
    history_cols = history[0:HISTORY_ROWS, :].rearrange("(p k) d -> p (k d)", p=P)
    x_rows = x.rearrange("(h l) d -> h (l d)", l=LO)
    table_rows = table.rearrange("(h l) d -> h (l d)", l=LO)
    out_rows = out.rearrange("(h l) d -> h (l d)", l=LO)

    with ExitStack() as ctx:
        def sb(name, shape, dt=F32):
            return ctx.enter_context(nc.sbuf_tensor(name, shape, dt))

        def ps(name, shape):
            return ctx.enter_context(nc.psum_tensor(name, shape, F32))

        def sem(name):
            return ctx.enter_context(nc.semaphore(name))

        x_sb = sb("x_sb", [P, LO, D])
        xT = sb("xT", [P, LO, HI])
        A = sb("A", [P, LO, D])
        M = sb("M", [P, LO, D])
        finite = sb("finite", [P, 2, OUT_W, D], I32)
        w_sb = sb("w_sb", [P, 2 * D])
        w_diff = sb("w_diff", [P, D])
        w2T = sb("w2T", [P, D])
        wdT = sb("wdT", [P, D])
        b_bc = sb("b_bc", [P, D])
        ident = sb("ident", [P, P])
        before = sb("before", [P, P])
        digit_i = sb("digit_i", [P, P], I32)
        digit = sb("digit", [P, P], BF16)
        zeros = sb("zeros", [P, P], BF16)
        eps = sb("eps", [P, 1])
        src_sb = sb("src_sb", [P, EDGE_COLS], I32)
        dst_i = sb("dst_i", [P, EDGE_COLS + 2], I32)
        dst_f = sb("dst_f", [P, EDGE_COLS + 2])
        change = sb("change", [P, EDGE_COLS + 1])
        col_i = sb("col_i", [P, EDGE_COLS], I32)
        work = sb("work", [P, EDGE_COLS])
        hi_bf = sb("hi_bf", [P, EDGE_COLS], BF16)
        lo_bf = sb("lo_bf", [P, EDGE_COLS], BF16)
        stage = [sb(f"stage{i}", [P, U], I32) for i in range(2)]
        rows = [sb(f"rows{i}", [P, U, D]) for i in range(2)]
        running = [sb(f"running{i}", [P, U, D]) for i in range(2)]
        hot_hi = [sb(f"hot_hi{i}", [P, U, HI], BF16) for i in range(2)]
        hot_lo = [sb(f"hot_lo{i}", [P, U, LO], BF16) for i in range(2)]
        count = sb("count", [P, LO])
        upto = sb("upto", [P, LO])
        rowsum = sb("rowsum", [P, 1])
        offset = sb("offset", [P, 1])
        end_idx = sb("end_idx", [P, LO], I32)
        nonempty = sb("nonempty", [P, LO])
        ones_lo = sb("ones_lo", [P, LO])
        flags = sb("flags", [P, 2])
        caps = sb("caps", [P, 2])
        full_bc = sb("full_bc", [P, P])
        full_capT = sb("full_capT", [P, P])
        first_end = sb("first_end", [P, 1])
        has_end = sb("has_end", [P, 1])
        base_i = sb("base_i", [P, 2], I32)
        base_f = sb("base_f", [P, 2])
        fix_from = sb("fix_from", [P, 1])
        fix_to = sb("fix_to", [P, 1])
        fix_from_i = sb("fix_from_i", [P, 1], I32)
        fix_to_i = sb("fix_to_i", [P, 1], I32)
        fix_rows = sb("fix_rows", [P, D])
        fixed = sb("fixed", [P, D])
        carryT = sb("carryT", [P, P + 1])
        stats = sb("stats", [P, LO, 6])
        mean_var = sb("mean_var", [P, LO, 2])
        std = sb("std", [P, LO])
        rstd = sb("rstd", [P, LO])
        shift = sb("shift", [P, LO])

        p_xT = [ps(f"p_xT{i}", [P, 512]) for i in range(2)]
        p_B = [ps(f"p_B{i}", [P, 512]) for i in range(2)]
        p_w = ps("p_w", [P, 512])
        p_count = ps("p_count", [P, 512])
        p_small = ps("p_small", [P, 512])
        p_carry = ps("p_carry", [P, 512])

        s_const = sem("s_const")
        s_x = [sem(f"s_x{c}") for c in range(CHUNKS)]
        s_w = sem("s_w")
        s_edges_clear = sem("s_edges_clear")
        s_edges = sem("s_edges")
        s_wdiff = sem("s_wdiff")
        s_pw = sem("s_pw")
        s_wT = sem("s_wT")
        s_pxT = sem("s_pxT")
        s_xT = sem("s_xT")
        s_pB = sem("s_pB")
        s_B = sem("s_B")
        s_pA = sem("s_pA")
        s_A = sem("s_A")
        s_table = sem("s_table")
        s_dve = sem("s_dve")
        s_fullbc = sem("s_fullbc")
        s_pfull = sem("s_pfull")
        s_staged = sem("s_staged")
        s_go = sem("s_go")
        s_rows = [sem(f"s_rows{i}") for i in range(2)]
        s_steps = sem("s_steps")
        s_hot = sem("s_hot")
        s_counted = sem("s_counted")
        s_history = [sem(f"s_history{i}") for i in range(2)]
        s_rowsum = sem("s_rowsum")
        s_poffset = sem("s_poffset")
        s_ends = sem("s_ends")
        s_fix_read = sem("s_fix_read")
        s_pT = sem("s_pT")
        s_carryT = sem("s_carryT")
        s_pcarry = sem("s_pcarry")
        s_fixed = sem("s_fixed")
        s_fix_written = sem("s_fix_written")
        s_max = [sem(f"s_max{c}") for c in range(OUTS)]
        s_var = sem("s_var")
        s_std = sem("s_std")
        s_shift = sem("s_shift")
        s_normed = sem("s_normed")
        s_out = sem("s_out")

        block = ctx.enter_context(nc.Block())
        LAST = (BLOCKS - 1) % 2

        def group_lo(g):
            return g * GROUP, min((g + 1) * GROUP, LO)

        def chunk_of(g):
            return max(c for c in range(CHUNKS) if CHUNK_GROUPS[c] <= g)

        @block.sync
        def _(sp):
            sp.dma_start(w_sb[:, :], W).then_inc(s_w, 16)
            sp.dma_start(b_bc[:, :], b.rearrange("(a d) -> a d", a=1).to_broadcast([P, D])).then_inc(s_w, 16)
            for c in range(CHUNKS):
                for h0, h1 in HI_SPLIT:
                    sp.dma_start(x_sb[h0:h1, CHUNK_LO[c]:CHUNK_LO[c + 1], :],
                                 x_rows[h0:h1, CHUNK_LO[c] * D:CHUNK_LO[c + 1] * D]).then_inc(s_x[c], 16)
            sp.wait_ge(s_edges_clear, 3)
            src_main = src[0:(P - 1) * EDGE_COLS].rearrange("(p k) -> p k", k=EDGE_COLS)
            for p0, p1 in EDGE_SPLIT:
                sp.dma_start(src_sb[p0:p1, :], src_main[p0:p1, :]).then_inc(s_edges, 16)
            sp.dma_start(src_sb[P - 1:P, 0:LAST_COLS],
                         src[(P - 1) * EDGE_COLS:E].rearrange("(a k) -> a k", a=1)).then_inc(s_edges, 16)
            dst_main = dst[0:(P - 1) * EDGE_COLS].rearrange("(p k) -> p k", k=EDGE_COLS)
            dst_next = dst[EDGE_COLS:EDGE_COLS * P - EDGE_COLS].rearrange("(p k) -> p k", k=EDGE_COLS)
            for p0, p1 in EDGE_SPLIT:
                sp.dma_start(dst_i[p0:p1, 1:EDGE_COLS + 1], dst_main[p0:p1, :]).then_inc(s_edges, 16)
            sp.dma_start(dst_i[P - 1:P, 1:LAST_COLS + 1],
                         dst[(P - 1) * EDGE_COLS:E].rearrange("(a k) -> a k", a=1)).then_inc(s_edges, 16)
            sp.dma_start(dst_i[1:P, 0:1], dst_main[0:P - 1, EDGE_COLS - 1:EDGE_COLS],
                         allow_slow_non_contiguous=True).then_inc(s_edges, 16)
            sp.dma_start(dst_i[0:P - 2, EDGE_COLS + 1:EDGE_COLS + 2], dst_next[:, 0:1],
                         allow_slow_non_contiguous=True).then_inc(s_edges, 16)
            sp.dma_start(dst_i[P - 2:P - 1, EDGE_COLS + 1:EDGE_COLS + 2],
                         dst[(P - 1) * EDGE_COLS:(P - 1) * EDGE_COLS + 1].rearrange("(a k) -> a k", a=1)
                         ).then_inc(s_edges, 16)

            for c in range(CHUNKS):
                sp.wait_ge(s_B, CHUNK_GROUPS[c + 1])
                for h0, h1 in HI_SPLIT:
                    sp.dma_start(table_rows[h0:h1, CHUNK_LO[c] * D:CHUNK_LO[c + 1] * D],
                                 M[h0:h1, CHUNK_LO[c]:CHUNK_LO[c + 1], :]).then_inc(s_table, 16)

            def write_history(j, par):
                sp.wait_ge(s_steps, (j + 1) * U)
                sp.dma_start(history_cols[:, bass.ds(j * (U * D), U * D)],
                             running[par][:, :, :].rearrange("p u d -> p (u d)")).then_inc(s_history[par], 16)

            with sp.Fori(0, PAIRS) as i:
                for par in range(2):
                    write_history(i * 2 + par, par)

            for c in range(OUTS):
                l0, l1 = OUT_LO[c], OUT_LO[c + 1]
                sp.wait_ge(s_normed, l1)
                for h0, h1 in HI_SPLIT:
                    sp.dma_start(out_rows[h0:h1, l0 * D:l1 * D], M[h0:h1, l0:l1, :]).then_inc(s_out, 16)
            sp.wait_ge(s_out, 16 * len(HI_SPLIT) * OUTS)

        @block.gpsimd
        def _(pool):
            pool.memset(ident[:, :], 0.0).then_inc(s_const, 1)
            pool.memset(before[:, :], 0.0).then_inc(s_const, 1)
            pool.memset(src_sb[:, LAST_COLS:EDGE_COLS], 0).then_inc(s_edges_clear, 1)
            pool.memset(dst_i[:, LAST_COLS + 1:EDGE_COLS + 2], N).then_inc(s_edges_clear, 1)
            pool.memset(dst_i[:, 0:1], -1).then_inc(s_edges_clear, 1)
            pool.wait_ge(s_const, 2)
            pool.affine_select(out=ident[:, :], in_=ident[:, :], compare_op=ALU.not_equal, fill=1.0,
                               base=0, pattern=[[-1, P]], channel_multiplier=1).then_inc(s_const, 1)
            pool.affine_select(out=before[:, :], in_=before[:, :], compare_op=ALU.is_ge, fill=1.0,
                               base=0, pattern=[[-1, P]], channel_multiplier=1).then_inc(s_const, 1)
            pool.iota(digit_i[:, :], pattern=[[1, P]], base=0, channel_multiplier=0).then_inc(s_const, 1)
            pool.iota(col_i[:, :], pattern=[[1, EDGE_COLS]], base=0, channel_multiplier=0).then_inc(s_const, 1)
            pool.iota(base_i[:, 0:1], pattern=[[0, 1]], base=0, channel_multiplier=EDGE_COLS).then_inc(s_const, 1)
            pool.iota(base_i[:, 1:2], pattern=[[0, 1]], base=HISTORY_ROWS, channel_multiplier=1
                      ).then_inc(s_const, 1)

            pool.wait_ge(s_table, 16 * len(HI_SPLIT) * CHUNKS)

            def gather_rows(j, par, first):
                pool.wait_ge(s_staged, j + 1)
                if not first:
                    pool.wait_ge(s_steps, (j - 1) * U)
                pool.sem_inc(s_go, 1)
                for u in range(U):
                    pool.indirect_dma_start(
                        out=rows[par][:, u, :], out_offset=None, in_=table[:, :],
                        in_offset=bass.IndirectOffsetOnAxis(ap=stage[par][:, u:u + 1], axis=0),
                    ).then_inc(s_rows[par], 16)

            for par in range(2):
                gather_rows(par, par, True)
            with pool.Fori(1, PAIRS) as i:
                for par in range(2):
                    gather_rows(i * 2 + par, par, False)

            for par in range(2):
                pool.wait_ge(s_history[par], 16 * PAIRS)
            pool.wait_ge(s_ends, 1)
            pool.indirect_dma_start(
                out=fix_rows[:, :], out_offset=None, in_=history[0:HISTORY_ROWS, :],
                in_offset=bass.IndirectOffsetOnAxis(ap=fix_from_i[:, 0:1], axis=0)).then_inc(s_fix_read, 16)
            pool.wait_ge(s_fixed, 1)
            pool.indirect_dma_start(
                out=history[:, :], out_offset=bass.IndirectOffsetOnAxis(ap=fix_to_i[:, 0:1], axis=0),
                in_=fixed[:, :], in_offset=None).then_inc(s_fix_written, 16)
            pool.wait_ge(s_fix_written, 16)
            for c in range(OUTS):
                for l in range(OUT_LO[c], OUT_LO[c + 1]):
                    pool.indirect_dma_start(
                        out=M[:, l, :], out_offset=None, in_=history[0:HISTORY_ROWS, :],
                        in_offset=bass.IndirectOffsetOnAxis(ap=end_idx[:, l:l + 1], axis=0),
                    ).then_inc(s_max[c], 16)

        @block.scalar
        def _(act):
            for g in range(GROUPS):
                l0, l1 = group_lo(g)
                act.wait_ge(s_pB, g + 1)
                act.copy(M[0:HI, l0:l1, :].rearrange("p l d -> p (l d)"),
                         p_B[g % 2][0:HI, 0:(l1 - l0) * D]).then_inc(s_B, 1)

            def stage_block(j, i, par, first):
                if not first:
                    act.wait_ge(s_rows[par], i * (16 * U))
                act.copy(stage[par][:, :], src_sb[:, bass.ds(j * U, U)]).then_inc(s_staged, 1)

            act.wait_ge(s_edges, 16 * 9)
            for par in range(2):
                stage_block(par, 0, par, True)
            with act.Fori(1, PAIRS) as i:
                for par in range(2):
                    stage_block(i * 2 + par, i, par, False)

            for c in range(OUTS):
                l0, l1 = OUT_LO[c], OUT_LO[c + 1]
                act.wait_ge(s_var, c + 1)
                act.activation(std[0:HI, l0:l1], mean_var[0:HI, l0:l1, 1], ACT.Sqrt,
                               bias=eps[0:HI, 0:1]).then_inc(s_std, 1)
                act.wait_ge(s_shift, c + 1)
                for l in range(l0, l1):
                    act.activation(M[0:HI, l, :], x_sb[0:HI, l, :], ACT.Identity,
                                   scale=rstd[0:HI, l:l + 1], bias=shift[0:HI, l:l + 1]).then_inc(s_normed, 1)

        @block.tensor
        def _(pe):
            pe.wait_ge(s_const, 4)
            pe.wait_ge(s_wdiff, 1)
            pe.transpose(p_w[:, 0:D], w_sb[:, D:2 * D], ident[:, :]).then_inc(s_pw, 1)
            pe.transpose(p_w[:, D:2 * D], w_diff[:, :], ident[:, :]).then_inc(s_pw, 1)

            def transpose_x(g):
                l0, l1 = group_lo(g)
                for h in range(len(HI_SPLIT)):
                    pe.wait_ge(s_x[chunk_of(g)], 16 * len(HI_SPLIT))
                if g >= 2:
                    pe.wait_ge(s_xT, g - 1)
                for l in range(l0, l1):
                    mm = pe.transpose(p_xT[g % 2][:, (l - l0) * HI:(l - l0 + 1) * HI],
                                      x_sb[0:HI, l, :], ident[0:HI, 0:HI])
                mm.then_inc(s_pxT, 1)

            def project_B(g):
                l0, l1 = group_lo(g)
                pe.wait_ge(s_xT, g + 1)
                if g == 0:
                    pe.wait_ge(s_wT, 2)
                if g >= 2:
                    pe.wait_ge(s_B, g - 1)
                for l in range(l0, l1):
                    mm = pe.matmul(p_B[g % 2][0:HI, (l - l0) * D:(l - l0 + 1) * D], xT[:, l, :], w2T[:, :],
                                   start=True, stop=True)
                mm.then_inc(s_pB, 1)

            def project_A(g):
                l0, l1 = group_lo(g)
                if g < 2:
                    pe.wait_ge(s_B, GROUPS)
                else:
                    pe.wait_ge(s_A, g - 1)
                for l in range(l0, l1):
                    mm = pe.matmul(p_B[g % 2][0:HI, (l - l0) * D:(l - l0 + 1) * D], xT[:, l, :], wdT[:, :],
                                   start=True, stop=True)
                mm.then_inc(s_pA, 1)

            transpose_x(0)
            for g in range(GROUPS):
                if g + 1 < GROUPS:
                    transpose_x(g + 1)
                project_B(g)
            for g in range(GROUPS):
                project_A(g)

            pe.wait_ge(s_fullbc, 1)
            pe.transpose(p_small[:, 0:P], full_bc[:, :], ident[:, :]).then_inc(s_pfull, 1)

            pe.matmul(p_count[0:HI, 0:LO], zeros[:, 0:HI], zeros[:, 0:LO], start=True, stop=False,
                      skip_group_check=True)

            def count_block(j, par):
                pe.wait_ge(s_hot, (j + 1) * 2)
                for u in range(U):
                    mm = pe.matmul(p_count[0:HI, 0:LO], hot_hi[par][:, u, :], hot_lo[par][:, u, :],
                                   start=False, stop=False, skip_group_check=True)
                mm.then_inc(s_counted, 1)

            with pe.Fori(0, PAIRS) as i:
                for par in range(2):
                    count_block(i * 2 + par, par)

            pe.wait_ge(s_rowsum, 1)
            pe.matmul(p_small[0:HI, P:P + 1], before[0:HI, 0:HI], rowsum[0:HI, 0:1],
                      start=True, stop=True).then_inc(s_poffset, 1)

            pe.wait_ge(s_steps, EDGE_COLS)
            pe.transpose(p_carry[:, 0:P], running[LAST][:, U - 1, :], ident[:, :]).then_inc(s_pT, 1)
            pe.wait_ge(s_carryT, 1)
            pe.transpose(p_carry[:, P:2 * P], carryT[:, 0:P], ident[:, :]).then_inc(s_pcarry, 1)

        @block.vector
        def _(dve):
            done = [0]

            def chain(ins):
                done[0] += 1
                ins.then_inc(s_dve, 1)
                dve.wait_ge(s_dve, done[0])

            dve.memset(zeros[:, :], 0.0)
            dve.memset(eps[:, :], EPS)
            dve.memset(ones_lo[:, :], 1.0)
            dve.memset(end_idx[:, :], 0)
            dve.memset(carryT[:, 0:1], 0.0)
            chain(dve.memset(running[1][:, U - 1, :], 0.0))
            dve.wait_ge(s_w, 32)
            dve.tensor_tensor(w_diff[:, :], w_sb[:, 0:D], w_sb[:, D:2 * D], ALU.subtract).then_inc(s_wdiff, 1)
            dve.wait_ge(s_pw, 2)
            dve.tensor_copy(w2T[:, :], p_w[:, 0:D]).then_inc(s_wT, 1)
            dve.tensor_copy(wdT[:, :], p_w[:, D:2 * D]).then_inc(s_wT, 1)

            for g in range(GROUPS):
                l0, l1 = group_lo(g)
                dve.wait_ge(s_pxT, g + 1)
                dve.tensor_copy(xT[:, l0:l1, :].rearrange("p l h -> p (l h)"),
                                p_xT[g % 2][:, 0:(l1 - l0) * HI]).then_inc(s_xT, 1)

            dve.wait_ge(s_edges, 16 * 9)
            chain(dve.tensor_copy(dst_f[:, :], dst_i[:, :]))
            chain(dve.tensor_tensor(change[:, :], dst_f[:, 1:EDGE_COLS + 2], dst_f[:, 0:EDGE_COLS + 1],
                                    ALU.not_equal))
            dve.tensor_reduce(flags[:, 1:2], change[:, 0:EDGE_COLS], AX_X, ALU.max)
            dve.wait_ge(s_const, 8)
            chain(dve.tensor_copy(work[:, :], col_i[:, :]))
            chain(dve.scalar_tensor_tensor(out=work[:, :], in0=change[:, 1:EDGE_COLS + 1], scalar=-FAR,
                                           in1=work[:, :], op0=ALU.mult, op1=ALU.add))
            dve.tensor_reduce(first_end[:, :], work[:, :], AX_X, ALU.min)
            chain(dve.tensor_copy(flags[:, 0:1], change[:, 0:1]))
            chain(dve.memset(change[:, 0:1], 1.0))
            for t in (change, flags):
                o = caps if t is flags else change
                chain(dve.tensor_scalar(o[:, :], t[:, :], -2.0, 1.0, ALU.mult, ALU.add))
                chain(dve.tensor_scalar(o[:, :], o[:, :], F32_MAX, None, ALU.mult))
            dve.tensor_copy(full_bc[:, :], caps[:, 1:2].to_broadcast([P, P])).then_inc(s_fullbc, 1)
            chain(dve.tensor_copy(base_f[:, :], base_i[:, :]))
            chain(dve.tensor_scalar(has_end[:, :], first_end[:, :], 0.0, None, ALU.is_lt))
            chain(dve.scalar_tensor_tensor(out=first_end[:, :], in0=has_end[:, :], scalar=FAR,
                                           in1=first_end[:, :], op0=ALU.mult, op1=ALU.add))
            chain(dve.tensor_tensor(fix_from[:, :], first_end[:, :], base_f[:, 0:1], ALU.add))
            chain(dve.tensor_tensor(fix_to[:, :], fix_from[:, :], base_f[:, 1:2], ALU.subtract))
            chain(dve.scalar_tensor_tensor(out=fix_to[:, :], in0=fix_to[:, :], scalar=has_end[:, 0:1],
                                           in1=base_f[:, 1:2], op0=ALU.mult, op1=ALU.add))
            dve.tensor_copy(fix_from_i[:, :], fix_from[:, :])
            dve.tensor_copy(fix_to_i[:, :], fix_to[:, :])

            dst_own = dst_f[:, 1:EDGE_COLS + 1]
            dve.tensor_copy(digit[:, :], digit_i[:, :])
            chain(dve.tensor_scalar(work[:, :], dst_own, (LO - 1) / 2.0, 1.0 / LO, ALU.subtract, ALU.mult))
            chain(dve.tensor_scalar(work[:, :], work[:, :], ROUND, None, ALU.add))
            chain(dve.tensor_scalar(work[:, :], work[:, :], ROUND, None, ALU.subtract))
            dve.tensor_copy(hi_bf[:, :], work[:, :])
            chain(dve.scalar_tensor_tensor(out=lo_bf[:, :], in0=work[:, :], scalar=-float(LO), in1=dst_own,
                                           op0=ALU.mult, op1=ALU.add))

            for g in range(GROUPS):
                l0, l1 = group_lo(g)
                dve.wait_ge(s_pA, g + 1)
                dve.tensor_tensor(A[0:HI, l0:l1, :],
                                  p_B[g % 2][0:HI, 0:(l1 - l0) * D].rearrange("p (l d) -> p l d", d=D),
                                  b_bc[0:HI, :].unsqueeze(1).to_broadcast([HI, l1 - l0, D]),
                                  ALU.add).then_inc(s_A, 1)
            dve.wait_ge(s_pfull, 1)
            chain(dve.tensor_copy(full_capT[:, :], p_small[:, 0:P]))

            def one_hots(j, par, first):
                if not first:
                    dve.wait_ge(s_counted, j - 1)
                for hot, dig, width in ((hot_hi, hi_bf, HI), (hot_lo, lo_bf, LO)):
                    dve.tensor_tensor(hot[par][:, :, :],
                                      dig[:, bass.ds(j * U, U)].unsqueeze(2).to_broadcast([P, U, width]),
                                      digit[:, 0:width].unsqueeze(1).to_broadcast([P, U, width]),
                                      ALU.is_equal).then_inc(s_hot, 1)

            def fold(j, i, par, first):
                dve.wait_ge(s_rows[par], (i + 1) * (16 * U))
                if not first:
                    dve.wait_ge(s_history[par], i * 16)
                for u in range(U):
                    before_row = running[par][:, u - 1, :] if u else running[1 - par][:, U - 1, :]
                    if not (first and par == 0 and u == 0):
                        dve.wait_ge(s_steps, j * U + u)
                    dve.scalar_tensor_tensor(out=running[par][:, u, :], in0=before_row,
                                             scalar=change[:, bass.ds(j * U + u, 1)],
                                             in1=rows[par][:, u, :], op0=ALU.min, op1=ALU.max
                                             ).then_inc(s_steps, 1)

            for par in range(2):
                one_hots(par, par, True)
                fold(par, 0, par, True)
            with dve.Fori(1, PAIRS - 1) as i:
                for par in range(2):
                    one_hots(i * 2 + par, par, False)
                    fold(i * 2 + par, i, par, False)
            for par in range(2):
                one_hots(BLOCKS - 2 + par, par, False)
            fold(BLOCKS - 2, PAIRS - 1, 0, False)

            dve.wait_ge(s_counted, BLOCKS)
            chain(dve.tensor_copy(count[0:HI, :], p_count[0:HI, 0:LO]))
            chain(dve.tensor_tensor_scan(upto[0:HI, :], ones_lo[0:HI, :], count[0:HI, :], 0.0,
                                         ALU.mult, ALU.add))
            dve.tensor_copy(rowsum[0:HI, :], upto[0:HI, LO - 1:LO]).then_inc(s_rowsum, 1)
            dve.wait_ge(s_poffset, 1)
            chain(dve.tensor_copy(offset[0:HI, :], p_small[0:HI, P:P + 1]))
            chain(dve.tensor_scalar(upto[0:HI, :], upto[0:HI, :], offset[0:HI, 0:1], -1.0, ALU.add, ALU.add))
            chain(dve.tensor_scalar(end_idx[0:HI, :], upto[0:HI, :], 0.0, None, ALU.max))
            chain(dve.tensor_scalar(nonempty[0:HI, :], count[0:HI, :], 0.0, None, ALU.is_gt))
            chain(dve.tensor_scalar(nonempty[0:HI, :], nonempty[0:HI, :], 2.0, -1.0, ALU.mult, ALU.add))
            chain(dve.tensor_scalar(nonempty[0:HI, :], nonempty[0:HI, :], F32_MAX, None, ALU.mult))
            dve.tensor_tensor(A[0:HI, :, :], A[0:HI, :, :],
                              nonempty[0:HI, :].unsqueeze(2).to_broadcast([HI, LO, D]),
                              ALU.min).then_inc(s_ends, 1)

            fold(BLOCKS - 1, PAIRS - 1, 1, False)

            dve.wait_ge(s_pT, 1)
            dve.tensor_tensor_scan(carryT[:, 1:P + 1], full_capT[:, :], p_carry[:, 0:P], 0.0,
                                   ALU.min, ALU.max).then_inc(s_carryT, 1)
            dve.wait_ge(s_pcarry, 1)
            dve.wait_ge(s_fix_read, 16)
            dve.scalar_tensor_tensor(out=fixed[:, :], in0=p_carry[:, P:2 * P], scalar=caps[:, 0:1],
                                     in1=fix_rows[:, :], op0=ALU.min, op1=ALU.max).then_inc(s_fixed, 1)

            for c in range(OUTS):
                l0, l1 = OUT_LO[c], OUT_LO[c + 1]
                m, xs = M[0:HI, l0:l1, :], x_sb[0:HI, l0:l1, :]
                ok = finite[0:HI, c % 2, 0:l1 - l0, :]
                dve.wait_ge(s_max[c], 16 * (l1 - l0))
                chain(dve.tensor_tensor(m, m, A[0:HI, l0:l1, :], ALU.add))
                chain(dve.tensor_scalar(ok, m, -F32_MAX, None, ALU.is_gt))
                chain(dve.scalar_tensor_tensor(out=ok, in0=m, scalar=F32_MAX, in1=ok,
                                               op0=ALU.is_lt, op1=ALU.mult))
                chain(dve.tensor_tensor(m, m, xs, ALU.add))
                chain(dve.copy_predicated(xs, ok, m))
                for l in range(l0, l1):
                    s = dve.bn_stats(stats[0:HI, l, :], x_sb[0:HI, l, :])
                chain(s)
                for l in range(l0, l1):
                    s = dve.bn_aggr(mean_var[0:HI, l, :], stats[0:HI, l, :])
                s.then_inc(s_var, 1)
                dve.wait_ge(s_std, c + 1)
                chain(dve.reciprocal(rstd[0:HI, l0:l1], std[0:HI, l0:l1]))
                dve.scalar_tensor_tensor(out=shift[0:HI, l0:l1], in0=mean_var[0:HI, l0:l1, 0], scalar=-1.0,
                                         in1=rstd[0:HI, l0:l1], op0=ALU.mult, op1=ALU.mult).then_inc(s_shift, 1)


_INS = ['x', 'src', 'dst', 'L0_gnn_W', 'L0_gnn_b']
_OUTS = [((6250, 128), 'float32')]


def kernel(**inputs):
    import numpy as np
    import concourse.bacc as bacc
    from concourse.bass_utils import run_bass_kernel_spmd

    nc = bacc.Bacc("TRN2", target_bir_lowering=False, num_devices=1)
    arrays, args = {}, []
    for name in _INS:
        a = np.ascontiguousarray(inputs[name])
        arrays[f"in_{name}_dram"] = a
        args.append(nc.dram_tensor(f"in_{name}_dram", a.shape, mybir.dt.from_np(a.dtype), kind="ExternalInput").ap())
    for i, (shape, dtype) in enumerate(_OUTS):
        args.append(nc.dram_tensor(f"out_{i}_dram", shape, mybir.dt.from_np(np.dtype(dtype)), kind="ExternalOutput").ap())
    build(nc, *args)
    r = run_bass_kernel_spmd(nc, [arrays], core_ids=[0])
    return r.results[0]["out_0_dram"]
```

```python
from contextlib import ExitStack

import concourse.bass as bass
from concourse import mybir

P = 128
F32 = mybir.dt.float32
BF16 = mybir.dt.bfloat16
I32 = mybir.dt.int32
I16 = mybir.dt.int16
ALU = mybir.AluOpType
ACT = mybir.ActivationFunctionType
AX_X = mybir.AxisListType.X

F32_MAX = 3.4028234663852886e38
ROUND = 12582912.0
FAR = float(1 << 20)
EPS = 1e-5


def largest_divisor(n, most):
    return max(d for d in range(1, most + 1) if n % d == 0)


def build(nc, x, src, dst, W, b, out):
    N, D = x.shape
    E, = src.shape
    HI = largest_divisor(N, P - 1)
    LO = N // HI
    EDGE_COLS = -(-E // P)
    LAST_COLS = E - (P - 1) * EDGE_COLS
    U = largest_divisor(EDGE_COLS // 2, 16)
    GU = U - 1
    BLOCKS = EDGE_COLS // U
    PAIRS = BLOCKS // 2
    PICKED = BLOCKS - 2
    assert PAIRS * 2 * U == EDGE_COLS and 0 < LAST_COLS <= EDGE_COLS and D == P
    HISTORY_ROWS = P * EDGE_COLS
    LOWEST_ROW = HISTORY_ROWS
    SPARE_ROW = HISTORY_ROWS + 1
    GROUP = 4
    GROUPS = -(-LO // GROUP)
    CHUNK_GROUPS = [0, 2, 5, 8, 11, GROUPS]
    CHUNKS = len(CHUNK_GROUPS) - 1
    CHUNK_LO = [min(g * GROUP, LO) for g in CHUNK_GROUPS]
    HOTS = 5
    HOT_LO = LO // HOTS
    HALF = P // 2
    TAIL = 4
    HI_SPLIT = [(0, HI // 16 * 16), (HI // 16 * 16, HI)]
    EDGE_SPLIT = [(0, 112), (112, P - 1)]
    EDGE_LOADS = 2 * len(EDGE_SPLIT) + 5

    table = nc.dram_tensor("table", [N, D], F32, kind="Internal").ap()
    history = nc.dram_tensor("history", [SPARE_ROW + P, D], F32, kind="Internal").ap()
    history_cols = history[0:HISTORY_ROWS, :].rearrange("(p k) d -> p (k d)", p=P)
    x_rows = x.rearrange("(h l) d -> h (l d)", l=LO)
    table_rows = table.rearrange("(h l) d -> h (l d)", l=LO)
    out_rows = out.rearrange("(h l) d -> h (l d)", l=LO)

    with ExitStack() as ctx:
        def sb(name, shape, dt=F32):
            return ctx.enter_context(nc.sbuf_tensor(name, shape, dt))

        def ps(name, shape):
            return ctx.enter_context(nc.psum_tensor(name, shape, F32))

        def sem(name):
            return ctx.enter_context(nc.semaphore(name))

        x_sb = sb("x_sb", [P, LO, D])
        parts01 = x_sb[:, :, :].rearrange("p l d -> p (l d)").bitcast(BF16).rearrange(
            "p (s l d) -> p s l d", s=2, d=D)
        part2 = sb("part2", [P, LO, D], BF16)
        parts = [parts01[:, 0], parts01[:, 1], part2[:, :, :]]
        xT = sb("xT", [P, LO, HI])
        M = sb("M", [P, LO, D])
        w_sb = sb("w_sb", [P, 2 * D])
        w_diff = sb("w_diff", [P, D])
        w2T = sb("w2T", [P, D])
        wdT = sb("wdT", [P, D])
        b_row = sb("b_row", [1, GROUP * D])
        one_row = sb("one_row", [1, P])
        lowest = sb("lowest", [1, D])
        ident = sb("ident", [P, P])
        before = sb("before", [P, P])
        digit_i = sb("digit_i", [P, P], I32)
        digit = sb("digit", [P, P], BF16)
        zeros = sb("zeros", [P, P], BF16)
        eps = sb("eps", [P, 1])
        node_i = sb("node_i", [P, LO], I32)
        node = sb("node", [P, LO, HALF], I16)
        src_sb = sb("src_sb", [P, EDGE_COLS], I32)
        dst_f = sb("dst_f", [P, EDGE_COLS + 2])
        dst_i = dst_f[:, :].bitcast(I32)
        change = sb("change", [P, EDGE_COLS + 1])
        work = sb("work", [P, EDGE_COLS])
        col_i = work[:, :].bitcast(I32)
        hi_bf = sb("hi_bf", [P, EDGE_COLS], BF16)
        lo_bf = sb("lo_bf", [P, EDGE_COLS], BF16)
        stage = [sb(f"stage{i}", [P, U], I32) for i in range(2)]
        rows = [sb(f"rows{i}", [P, U, D]) for i in range(2)]
        running = [sb(f"running{i}", [P, U, D]) for i in range(2)]
        hot_hi = [sb(f"hot_hi{i}", [P, U, HI], BF16) for i in range(2)]
        hot_lo = [sb(f"hot_lo{i}", [P, U, LO], BF16) for i in range(2)]
        src_wide = sb("src_wide", [P, P])
        src_row = [sb(f"src_row{i}", [P, P], I16) for i in range(2)]
        hot_src = sb("hot_src", [P, 2, LO, P], BF16)
        size = rows[0][:, 0:2 * GROUP, :].rearrange("p (s u) d -> p s (u d)", s=2)
        finite = rows[1][:, :, :].rearrange("p u d -> p (u d)").bitcast(I32)
        y = running[0][:, :, :].rearrange("p u d -> p (u d)")
        count = sb("count", [P, LO])
        upto = sb("upto", [P, LO])
        rowsum = sb("rowsum", [P, 1])
        offset = sb("offset", [P, 1])
        end_idx = sb("end_idx", [P, LO], I32)
        nonempty = sb("nonempty", [P, LO])
        ones_lo = sb("ones_lo", [P, LO])
        flags = sb("flags", [P, 2])
        caps = sb("caps", [P, 2])
        full_bc = sb("full_bc", [P, P])
        full_capT = sb("full_capT", [P, P])
        first_end = sb("first_end", [P, 1])
        has_end = sb("has_end", [P, 1])
        base_i = sb("base_i", [P, 2], I32)
        base_f = sb("base_f", [P, 2])
        fix_from = sb("fix_from", [P, 1])
        fix_to = sb("fix_to", [P, 1])
        fix_from_i = sb("fix_from_i", [P, 1], I32)
        fix_to_i = sb("fix_to_i", [P, 1], I32)
        fix_rows = sb("fix_rows", [P, D])
        fixed = sb("fixed", [P, D])
        carryT = sb("carryT", [P, P + 1])
        stats = sb("stats", [P, LO, 6])
        mean_var = sb("mean_var", [P, LO, 2])
        std = sb("std", [P, LO])
        rstd = sb("rstd", [P, LO])
        shift = sb("shift", [P, LO])

        p_xT = [ps(f"p_xT{i}", [P, 512]) for i in range(2)]
        p_picked = p_xT
        p_B = [ps(f"p_B{i}", [P, 512]) for i in range(2)]
        p_A = p_B
        p_w = ps("p_w", [P, 512])
        p_src = p_w
        p_count = ps("p_count", [P, 512])
        p_small = ps("p_small", [P, 512])
        p_carry = ps("p_carry", [P, 512])

        s_const = sem("s_const")
        s_x = [sem(f"s_x{c}") for c in range(CHUNKS)]
        s_x_again = sem("s_x_again")
        s_w = sem("s_w")
        s_edges_clear = sem("s_edges_clear")
        s_edges = sem("s_edges")
        s_node_i = sem("s_node_i")
        s_node = sem("s_node")
        s_dst = sem("s_dst")
        s_change = sem("s_change")
        s_wdiff = sem("s_wdiff")
        s_pw = sem("s_pw")
        s_wT = sem("s_wT")
        s_pxT = sem("s_pxT")
        s_xT = sem("s_xT")
        s_pB = sem("s_pB")
        s_B = sem("s_B")
        s_part = [sem(f"s_part{i}") for i in range(3)]
        s_rest = [sem(f"s_rest{i}") for i in range(2)]
        s_pA = sem("s_pA")
        s_A = sem("s_A")
        s_table = [sem(f"s_table{c}") for c in range(CHUNKS)]
        s_dve = sem("s_dve")
        s_lowest = sem("s_lowest")
        s_lowest_out = sem("s_lowest_out")
        s_fullbc = sem("s_fullbc")
        s_pfull = sem("s_pfull")
        s_staged = sem("s_staged")
        s_go = sem("s_go")
        s_rows = [sem(f"s_rows{i}") for i in range(2)]
        s_rows_tail = [sem(f"s_rows_tail{i}") for i in range(-(-GU // TAIL))]
        s_steps = sem("s_steps")
        s_hot = sem("s_hot")
        s_counted = sem("s_counted")
        s_wide = sem("s_wide")
        s_psrc = sem("s_psrc")
        s_src_row = sem("s_src_row")
        s_hot_src = sem("s_hot_src")
        s_picked = sem("s_picked")
        s_history = [sem(f"s_history{i}") for i in range(2)]
        s_rowsum = sem("s_rowsum")
        s_poffset = sem("s_poffset")
        s_ends = sem("s_ends")
        s_fix_read = sem("s_fix_read")
        s_pT = sem("s_pT")
        s_carryT = sem("s_carryT")
        s_pcarry = sem("s_pcarry")
        s_fixed = sem("s_fixed")
        s_fix_written = sem("s_fix_written")
        s_max = [sem(f"s_max{g}") for g in range(GROUPS)]
        s_sum = sem("s_sum")
        s_y = sem("s_y")
        s_size = sem("s_size")
        s_finite = sem("s_finite")
        s_var = sem("s_var")
        s_std = sem("s_std")
        s_shift = sem("s_shift")
        s_normed = sem("s_normed")
        s_out = sem("s_out")

        block = ctx.enter_context(nc.Block())
        LAST = (BLOCKS - 1) % 2

        def group_lo(g):
            return g * GROUP, min((g + 1) * GROUP, LO)

        def chunk_of(g):
            return max(c for c in range(CHUNKS) if CHUNK_GROUPS[c] <= g)

        @block.sync
        def _(sp):
            sp.dma_start(w_sb[:, :], W).then_inc(s_w, 16)

            def load_x(c, done):
                for h0, h1 in HI_SPLIT:
                    sp.dma_start(x_sb[h0:h1, CHUNK_LO[c]:CHUNK_LO[c + 1], :],
                                 x_rows[h0:h1, CHUNK_LO[c] * D:CHUNK_LO[c + 1] * D]).then_inc(done, 16)

            for c in range(CHUNKS):
                load_x(c, s_x[c])
            sp.wait_ge(s_edges_clear, 3)
            dst_main = dst[0:(P - 1) * EDGE_COLS].rearrange("(p k) -> p k", k=EDGE_COLS)
            dst_next = dst[EDGE_COLS:EDGE_COLS * P - EDGE_COLS].rearrange("(p k) -> p k", k=EDGE_COLS)
            for p0, p1 in EDGE_SPLIT:
                sp.dma_start(dst_i[p0:p1, 1:EDGE_COLS + 1], dst_main[p0:p1, :]).then_inc(s_edges, 16)
            sp.dma_start(dst_i[P - 1:P, 1:LAST_COLS + 1],
                         dst[(P - 1) * EDGE_COLS:E].rearrange("(a k) -> a k", a=1)).then_inc(s_edges, 16)
            sp.dma_start(dst_i[1:P, 0:1], dst_main[0:P - 1, EDGE_COLS - 1:EDGE_COLS],
                         allow_slow_non_contiguous=True).then_inc(s_edges, 16)
            sp.dma_start(dst_i[0:P - 2, EDGE_COLS + 1:EDGE_COLS + 2], dst_next[:, 0:1],
                         allow_slow_non_contiguous=True).then_inc(s_edges, 16)
            sp.dma_start(dst_i[P - 2:P - 1, EDGE_COLS + 1:EDGE_COLS + 2],
                         dst[(P - 1) * EDGE_COLS:(P - 1) * EDGE_COLS + 1].rearrange("(a k) -> a k", a=1)
                         ).then_inc(s_edges, 16)
            src_main = src[0:(P - 1) * EDGE_COLS].rearrange("(p k) -> p k", k=EDGE_COLS)
            for p0, p1 in EDGE_SPLIT:
                sp.dma_start(src_sb[p0:p1, :], src_main[p0:p1, :]).then_inc(s_edges, 16)
            sp.dma_start(src_sb[P - 1:P, 0:LAST_COLS],
                         src[(P - 1) * EDGE_COLS:E].rearrange("(a k) -> a k", a=1)).then_inc(s_edges, 16)

            for c in range(CHUNKS):
                sp.wait_ge(s_B, CHUNK_GROUPS[c + 1])
                for h0, h1 in HI_SPLIT:
                    sp.dma_start(table_rows[h0:h1, CHUNK_LO[c] * D:CHUNK_LO[c + 1] * D],
                                 M[h0:h1, CHUNK_LO[c]:CHUNK_LO[c + 1], :]).then_inc(s_table[c], 16)
            for k in range(GROUP):
                sp.dma_start(b_row[0:1, k * D:(k + 1) * D], b.rearrange("(a d) -> a d", a=1)).then_inc(s_w, 16)
            sp.wait_ge(s_lowest, 1)
            sp.dma_start(history[LOWEST_ROW:LOWEST_ROW + 1, :], lowest[0:1, :]).then_inc(s_lowest_out, 16)

            def write_history(j, par):
                sp.wait_ge(s_steps, (j + 1) * U)
                sp.dma_start(history_cols[:, bass.ds(j * (U * D), U * D)],
                             running[par][:, :, :].rearrange("p u d -> p (u d)")).then_inc(s_history[par], 16)

            with sp.Fori(0, PAIRS - 1) as i:
                for par in range(2):
                    write_history(i * 2 + par, par)
            sp.wait_ge(s_picked, PICKED)
            for c in range(CHUNKS):
                load_x(c, s_x_again)
            for par in range(2):
                write_history(BLOCKS - 2 + par, par)

            for g in range(GROUPS):
                l0, l1 = group_lo(g)
                sp.wait_ge(s_normed, l1)
                for h0, h1 in HI_SPLIT:
                    sp.dma_start(out_rows[h0:h1, l0 * D:l1 * D], M[h0:h1, l0:l1, :]).then_inc(s_out, 16)
            sp.wait_ge(s_out, 16 * len(HI_SPLIT) * GROUPS)

        @block.gpsimd
        def _(pool):
            pool.memset(ident[:, :], 0.0).then_inc(s_const, 1)
            pool.memset(before[:, :], 0.0).then_inc(s_const, 1)
            pool.memset(dst_i[:, LAST_COLS + 1:EDGE_COLS + 2], N).then_inc(s_edges_clear, 1)
            pool.memset(dst_i[:, 0:1], -1).then_inc(s_edges_clear, 1)
            pool.memset(src_sb[:, LAST_COLS:EDGE_COLS], 0).then_inc(s_edges_clear, 1)
            pool.wait_ge(s_const, 2)
            pool.affine_select(out=ident[:, :], in_=ident[:, :], compare_op=ALU.not_equal, fill=1.0,
                               base=0, pattern=[[-1, P]], channel_multiplier=1).then_inc(s_const, 1)
            pool.affine_select(out=before[:, :], in_=before[:, :], compare_op=ALU.is_ge, fill=1.0,
                               base=0, pattern=[[-1, P]], channel_multiplier=1).then_inc(s_const, 1)
            pool.iota(digit_i[:, :], pattern=[[1, P]], base=0, channel_multiplier=0).then_inc(s_const, 1)
            pool.iota(col_i, pattern=[[1, EDGE_COLS]], base=0, channel_multiplier=0).then_inc(s_const, 1)
            pool.iota(base_i[:, 0:1], pattern=[[0, 1]], base=0, channel_multiplier=EDGE_COLS).then_inc(s_const, 1)
            pool.iota(base_i[:, 1:2], pattern=[[0, 1]], base=SPARE_ROW, channel_multiplier=1
                      ).then_inc(s_const, 1)
            pool.iota(node_i[:, :], pattern=[[1, LO]], base=0, channel_multiplier=LO).then_inc(s_node_i, 1)
            pool.wait_ge(s_node_i, 1)
            pool.tensor_copy(node[:, :, :], node_i[:, :].unsqueeze(2).to_broadcast([P, LO, HALF])
                             ).then_inc(s_node, 1)
            pool.wait_ge(s_edges, 16 * EDGE_LOADS)
            pool.tensor_copy(dst_f[:, :], dst_i[:, :]).then_inc(s_dst, 1)

            for c in range(CHUNKS):
                pool.wait_ge(s_table[c], 16 * len(HI_SPLIT))

            def gather_row(par, u, landed):
                pool.indirect_dma_start(
                    out=rows[par][:, u, :], out_offset=None, in_=table[:, :],
                    in_offset=bass.IndirectOffsetOnAxis(ap=stage[par][:, u:u + 1], axis=0),
                ).then_inc(landed, 16)

            def clear_to_gather(j):
                pool.wait_ge(s_staged, j + 1)
                pool.wait_ge(s_steps, (j - 1) * U)
                pool.sem_inc(s_go, 1)

            for par in range(2):
                pool.wait_ge(s_staged, par + 1)
                for u in range(U):
                    gather_row(par, u, s_rows[par])
            with pool.Fori(1, PAIRS - 1) as i:
                for par in range(2):
                    clear_to_gather(i * 2 + par)
                    for u in range(GU):
                        gather_row(par, u, s_rows[par])
            clear_to_gather(BLOCKS - 2)
            for u in range(GU):
                gather_row(0, u, s_rows[0])
            clear_to_gather(BLOCKS - 1)
            for u in range(GU):
                gather_row(1, u, s_rows_tail[u // TAIL])

            for par in range(2):
                pool.wait_ge(s_history[par], 16 * PAIRS)
            pool.wait_ge(s_lowest_out, 16)
            pool.wait_ge(s_ends, 1)
            pool.indirect_dma_start(
                out=fix_rows[:, :], out_offset=None, in_=history[0:HISTORY_ROWS, :],
                in_offset=bass.IndirectOffsetOnAxis(ap=fix_from_i[:, 0:1], axis=0)).then_inc(s_fix_read, 16)
            pool.wait_ge(s_fixed, 1)
            pool.indirect_dma_start(
                out=history[:, :], out_offset=bass.IndirectOffsetOnAxis(ap=fix_to_i[:, 0:1], axis=0),
                in_=fixed[:, :], in_offset=None).then_inc(s_fix_written, 16)
            pool.wait_ge(s_fix_written, 16)
            for g in range(GROUPS):
                l0, l1 = group_lo(g)
                for l in range(l0, l1):
                    pool.indirect_dma_start(
                        out=M[:, l, :], out_offset=None, in_=history[0:LOWEST_ROW + 1, :],
                        in_offset=bass.IndirectOffsetOnAxis(ap=end_idx[:, l:l + 1], axis=0),
                    ).then_inc(s_max[g], 16)

        @block.scalar
        def _(act):
            for g in range(GROUPS):
                l0, l1 = group_lo(g)
                act.wait_ge(s_pB, g + 1)
                act.copy(M[0:HI, l0:l1, :].rearrange("p l d -> p (l d)"),
                         p_B[g % 2][0:HI, 0:(l1 - l0) * D]).then_inc(s_B, 1)

            def stage_block(j, i, par, first):
                if not first:
                    act.wait_ge(s_rows[par], (i - 1) * (16 * GU) + 16 * U)
                act.copy(stage[par][:, :], src_sb[:, bass.ds(j * U, U)]).then_inc(s_staged, 1)

            def src_to_row(q, par):
                if isinstance(q, int) and q == 0:
                    pass
                else:
                    act.wait_ge(s_psrc, q)
                act.copy(src_wide[:, :], src_sb[:, bass.ds(q * U + (2 * U + GU), 1)].to_broadcast([P, P])
                         ).then_inc(s_wide, 1)
                act.wait_ge(s_psrc, q + 1)
                if not (isinstance(q, int) and q < 2):
                    act.wait_ge(s_hot_src, (q - 1) * HOTS)
                act.copy(src_row[par][:, :], p_src[:, 0:P]).then_inc(s_src_row, 1)

            act.wait_ge(s_edges, 16 * EDGE_LOADS)
            for par in range(2):
                stage_block(par, 0, par, True)

            act.wait_ge(s_pxT, GROUPS)
            act.wait_ge(s_B, GROUPS)
            for n in range(3):
                for c in range(CHUNKS):
                    l0, l1 = CHUNK_LO[c], CHUNK_LO[c + 1]
                    if n:
                        act.wait_ge(s_rest[n - 1], c + 1)
                    act.copy(parts[n][0:HI, l0:l1, :], M[0:HI, l0:l1, :]).then_inc(s_part[n], 1)

            for q in range(2):
                src_to_row(q, q)
            with act.Fori(1, PAIRS - 1) as i:
                for par in range(2):
                    stage_block(i * 2 + par, i, par, False)
                    src_to_row(i * 2 + par, par)
            for par in range(2):
                stage_block(BLOCKS - 2 + par, PAIRS - 1, par, False)

            def scale_and_shift(g):
                l0, l1 = group_lo(g)
                act.wait_ge(s_shift, g + 1)
                for l in range(l0, l1):
                    act.activation(M[0:HI, l, :], x_sb[0:HI, l, :], ACT.Identity,
                                   scale=rstd[0:HI, l:l + 1], bias=shift[0:HI, l:l + 1]).then_inc(s_normed, 1)

            for g in range(GROUPS):
                l0, l1 = group_lo(g)
                w = (l1 - l0) * D
                act.wait_ge(s_sum, g + 1)
                if g >= 2:
                    act.wait_ge(s_finite, g - 1)
                act.activation(size[0:HI, g % 2, 0:w], M[0:HI, l0:l1, :].rearrange("p l d -> p (l d)"),
                               ACT.Abs).then_inc(s_size, 1)
                if g:
                    scale_and_shift(g - 1)
                act.wait_ge(s_var, g + 1)
                act.activation(std[0:HI, l0:l1], mean_var[0:HI, l0:l1, 1], ACT.Sqrt,
                               bias=eps[0:HI, 0:1]).then_inc(s_std, 1)
            scale_and_shift(GROUPS - 1)

        @block.tensor
        def _(pe):
            pe.wait_ge(s_const, 4)
            pe.wait_ge(s_wdiff, 1)
            pe.transpose(p_w[:, 0:D], w_sb[:, D:2 * D], ident[:, :]).then_inc(s_pw, 1)
            pe.transpose(p_w[:, D:2 * D], w_diff[:, :], ident[:, :]).then_inc(s_pw, 1)

            def transpose_x(g):
                l0, l1 = group_lo(g)
                pe.wait_ge(s_x[chunk_of(g)], 16 * len(HI_SPLIT))
                if g >= 2:
                    pe.wait_ge(s_xT, g - 1)
                for l in range(l0, l1):
                    mm = pe.transpose(p_xT[g % 2][:, (l - l0) * HI:(l - l0 + 1) * HI],
                                      x_sb[0:HI, l, :], ident[0:HI, 0:HI])
                mm.then_inc(s_pxT, 1)

            def project_B(g):
                l0, l1 = group_lo(g)
                pe.wait_ge(s_xT, g + 1)
                if g == 0:
                    pe.wait_ge(s_wT, 2)
                if g >= 2:
                    pe.wait_ge(s_B, g - 1)
                for l in range(l0, l1):
                    mm = pe.matmul(p_B[g % 2][0:HI, (l - l0) * D:(l - l0 + 1) * D], xT[:, l, :], w2T[:, :],
                                   start=True, stop=True)
                mm.then_inc(s_pB, 1)

            transpose_x(0)
            for g in range(GROUPS):
                if g + 1 < GROUPS:
                    transpose_x(g + 1)
                project_B(g)

            def turn_src(q):
                pe.wait_ge(s_wide, q + 1)
                if not (isinstance(q, int) and q == 0):
                    pe.wait_ge(s_src_row, q)
                pe.transpose(p_src[:, 0:P], src_wide[:, :], ident[:, :]).then_inc(s_psrc, 1)

            def pick_rows(q, par):
                if not (isinstance(q, int) and q < 2):
                    pe.wait_ge(s_steps, (q + 1) * U)
                for l in range(LO):
                    if l % HOT_LO == 0:
                        pe.wait_ge(s_hot_src, q * HOTS + (l // HOT_LO + 1))
                    for n in range(3):
                        mm = pe.matmul(p_picked[par][:, 0:D], hot_src[0:HI, par, l, :], parts[n][0:HI, l, :],
                                       start=(l == 0 and n == 0), stop=(l == LO - 1 and n == 2))
                mm.then_inc(s_picked, 1)

            def count_block(j, par):
                pe.wait_ge(s_hot, (j + 1) * 2)
                for u in range(U):
                    mm = pe.matmul(p_count[0:HI, 0:LO], hot_hi[par][:, u, :], hot_lo[par][:, u, :],
                                   start=False, stop=False, skip_group_check=True)
                mm.then_inc(s_counted, 1)

            pe.matmul(p_count[0:HI, 0:LO], zeros[:, 0:HI], zeros[:, 0:LO], start=True, stop=False,
                      skip_group_check=True)
            turn_src(0)
            turn_src(1)
            pe.wait_ge(s_part[2], CHUNKS)
            pick_rows(0, 0)
            pe.wait_ge(s_fullbc, 1)
            pe.transpose(p_small[:, 0:P], full_bc[:, :], ident[:, :]).then_inc(s_pfull, 1)
            for par in range(2):
                count_block(par, par)

            def rows_and_counts(j, par):
                turn_src(j)
                count_block(j, par)
                pick_rows(j - 1, 1 - par)

            for par in range(2):
                rows_and_counts(2 + par, par)
            with pe.Fori(2, PAIRS - 1) as i:
                for par in range(2):
                    rows_and_counts(i * 2 + par, par)
            count_block(BLOCKS - 2, 0)
            count_block(BLOCKS - 1, 1)
            pick_rows(PICKED - 1, 1)

            pe.wait_ge(s_rowsum, 1)
            pe.matmul(p_small[0:HI, P:P + 1], before[0:HI, 0:HI], rowsum[0:HI, 0:1],
                      start=True, stop=True).then_inc(s_poffset, 1)

            pe.wait_ge(s_steps, EDGE_COLS)
            pe.transpose(p_carry[:, 0:P], running[LAST][:, U - 1, :], ident[:, :]).then_inc(s_pT, 1)
            pe.wait_ge(s_carryT, 1)
            pe.transpose(p_carry[:, P:2 * P], carryT[:, 0:P], ident[:, :]).then_inc(s_pcarry, 1)

            pe.wait_ge(s_w, 16 * (1 + GROUP))
            for g in range(GROUPS):
                l0, l1 = group_lo(g)
                if g >= 2:
                    pe.wait_ge(s_sum, g - 1)
                pe.matmul(p_A[g % 2][0:HI, 0:(l1 - l0) * D], one_row[0:1, 0:HI], b_row[0:1, 0:(l1 - l0) * D],
                          start=True, stop=False, skip_group_check=True)
                for l in range(l0, l1):
                    mm = pe.matmul(p_A[g % 2][0:HI, (l - l0) * D:(l - l0 + 1) * D], xT[:, l, :], wdT[:, :],
                                   start=False, stop=True, skip_group_check=True)
                mm.then_inc(s_pA, 1)

        @block.vector
        def _(dve):
            done = [0]

            def chain(ins):
                done[0] += 1
                ins.then_inc(s_dve, 1)
                dve.wait_ge(s_dve, done[0])

            dve.memset(lowest[:, :], -F32_MAX).then_inc(s_lowest, 1)
            dve.memset(zeros[:, :], 0.0)
            dve.memset(eps[:, :], EPS)
            dve.memset(ones_lo[:, :], 1.0)
            dve.memset(one_row[:, :], 1.0)
            dve.memset(end_idx[:, :], 0)
            dve.memset(carryT[:, 0:1], 0.0)
            chain(dve.memset(running[1][:, U - 1, :], 0.0))
            dve.wait_ge(s_w, 16)
            dve.tensor_tensor(w_diff[:, :], w_sb[:, 0:D], w_sb[:, D:2 * D], ALU.subtract).then_inc(s_wdiff, 1)
            dve.wait_ge(s_pw, 2)
            dve.tensor_copy(w2T[:, :], p_w[:, 0:D]).then_inc(s_wT, 1)
            dve.tensor_copy(wdT[:, :], p_w[:, D:2 * D]).then_inc(s_wT, 1)

            for g in range(GROUPS):
                l0, l1 = group_lo(g)
                dve.wait_ge(s_pxT, g + 1)
                dve.tensor_copy(xT[:, l0:l1, :].rearrange("p l h -> p (l h)"),
                                p_xT[g % 2][:, 0:(l1 - l0) * HI]).then_inc(s_xT, 1)

            dve.wait_ge(s_dst, 1)
            dve.wait_ge(s_const, 8)
            chain(dve.tensor_tensor(change[:, :], dst_f[:, 1:EDGE_COLS + 2], dst_f[:, 0:EDGE_COLS + 1],
                                    ALU.not_equal))
            chain(dve.tensor_copy(work[:, :], col_i))
            dve.tensor_reduce(flags[:, 1:2], change[:, 0:EDGE_COLS], AX_X, ALU.max)
            chain(dve.scalar_tensor_tensor(out=work[:, :], in0=change[:, 1:EDGE_COLS + 1], scalar=-FAR,
                                           in1=work[:, :], op0=ALU.mult, op1=ALU.add))
            dve.tensor_reduce(first_end[:, :], work[:, :], AX_X, ALU.min)
            chain(dve.tensor_copy(flags[:, 0:1], change[:, 0:1]))
            chain(dve.memset(change[:, 0:1], 1.0))
            for t in (change, flags):
                o = caps if t is flags else change
                chain(dve.tensor_scalar(o[:, :], t[:, :], -2.0, 1.0, ALU.mult, ALU.add))
                chain(dve.tensor_scalar(o[:, :], o[:, :], F32_MAX, None, ALU.mult))
            dve.tensor_copy(full_bc[:, :], caps[:, 1:2].to_broadcast([P, P])).then_inc(s_fullbc, 1)

            def subtract_part(n):
                for c in range(CHUNKS):
                    l0, l1 = CHUNK_LO[c], CHUNK_LO[c + 1]
                    dve.wait_ge(s_part[n], c + 1)
                    if n == 0:
                        dve.wait_ge(s_table[c], 16 * len(HI_SPLIT))
                    dve.tensor_tensor(M[0:HI, l0:l1, :], M[0:HI, l0:l1, :], parts[n][0:HI, l0:l1, :],
                                      ALU.subtract).then_inc(s_rest[n], 1)

            def one_hot_src(q, par):
                dve.wait_ge(s_src_row, q + 1)
                if not (isinstance(q, int) and q < 2):
                    dve.wait_ge(s_picked, q - 1)
                row = src_row[par][:, :].rearrange("p (a e) -> p a e", e=HALF)
                for h in range(HOTS):
                    l0 = h * HOT_LO
                    dve.tensor_tensor(
                        hot_src[:, par, l0:l0 + HOT_LO, :].rearrange("p l (a e) -> p l a e", e=HALF),
                        row.unsqueeze(1).to_broadcast([P, HOT_LO, 2, HALF]),
                        node[:, l0:l0 + HOT_LO, :].unsqueeze(2).to_broadcast([P, HOT_LO, 2, HALF]),
                        ALU.is_equal).then_inc(s_hot_src, 1)

            def one_hots_dst(j, par):
                if not (isinstance(j, int) and j < 2):
                    dve.wait_ge(s_counted, j - 1)
                for hot, dig, width in ((hot_hi, hi_bf, HI), (hot_lo, lo_bf, LO)):
                    dve.tensor_tensor(hot[par][:, :, :],
                                      dig[:, bass.ds(j * U, U)].unsqueeze(2).to_broadcast([P, U, width]),
                                      digit[:, 0:width].unsqueeze(1).to_broadcast([P, U, width]),
                                      ALU.is_equal).then_inc(s_hot, 1)

            def fold(j, i, par, tail=False):
                first = isinstance(j, int) and j < 2
                if not tail:
                    dve.wait_ge(s_rows[par], i * (16 * GU) + 16 * U)
                if not first:
                    dve.wait_ge(s_history[par], i * 16)
                for u in range(U):
                    earlier = running[par][:, u - 1, :] if u else running[1 - par][:, U - 1, :]
                    row = rows[par][:, u, :]
                    if tail and u < GU and u % TAIL == 0:
                        dve.wait_ge(s_rows_tail[u // TAIL], 16 * (min(u + TAIL, GU) - u))
                    if u == GU and not first:
                        dve.wait_ge(s_picked, j - 1)
                        row = p_picked[par][:, 0:D]
                    if not (first and j == 0 and u == 0):
                        dve.wait_ge(s_steps, j * U + u)
                    dve.scalar_tensor_tensor(out=running[par][:, u, :], in0=earlier,
                                             scalar=change[:, bass.ds(j * U + u, 1)],
                                             in1=row, op0=ALU.min, op1=ALU.max).then_inc(s_steps, 1)

            subtract_part(0)
            dst_own = dst_f[:, 1:EDGE_COLS + 1]
            dve.tensor_copy(digit[:, :], digit_i[:, :])
            chain(dve.tensor_scalar(work[:, :], dst_own, (LO - 1) / 2.0, 1.0 / LO, ALU.subtract, ALU.mult))
            chain(dve.tensor_scalar(work[:, :], work[:, :], ROUND, None, ALU.add))
            chain(dve.tensor_scalar(work[:, :], work[:, :], ROUND, None, ALU.subtract))
            subtract_part(1)
            fold(0, 0, 0)
            dve.wait_ge(s_node, 1)
            one_hot_src(0, 0)
            dve.tensor_copy(hi_bf[:, :], work[:, :])
            chain(dve.scalar_tensor_tensor(out=lo_bf[:, :], in0=work[:, :], scalar=-float(LO), in1=dst_own,
                                           op0=ALU.mult, op1=ALU.add))
            one_hots_dst(0, 0)
            fold(1, 0, 1)
            one_hots_dst(1, 1)

            def block_work(j, i, par):
                one_hot_src(j - 1, 1 - par)
                fold(j, i, par)
                one_hots_dst(j + 2, par)

            for par in range(2):
                one_hots_dst(2 + par, par)
            for par in range(2):
                block_work(2 + par, 1, par)

            chain(dve.tensor_copy(base_f[:, :], base_i[:, :]))
            chain(dve.tensor_scalar(has_end[:, :], first_end[:, :], 0.0, None, ALU.is_lt))
            chain(dve.scalar_tensor_tensor(out=first_end[:, :], in0=has_end[:, :], scalar=FAR,
                                           in1=first_end[:, :], op0=ALU.mult, op1=ALU.add))
            chain(dve.tensor_tensor(fix_from[:, :], first_end[:, :], base_f[:, 0:1], ALU.add))
            chain(dve.tensor_tensor(fix_to[:, :], fix_from[:, :], base_f[:, 1:2], ALU.subtract))
            chain(dve.scalar_tensor_tensor(out=fix_to[:, :], in0=fix_to[:, :], scalar=has_end[:, 0:1],
                                           in1=base_f[:, 1:2], op0=ALU.mult, op1=ALU.add))
            dve.tensor_copy(fix_from_i[:, :], fix_from[:, :])
            chain(dve.tensor_copy(fix_to_i[:, :], fix_to[:, :]))
            dve.wait_ge(s_pfull, 1)
            chain(dve.tensor_copy(full_capT[:, :], p_small[:, 0:P]))

            with dve.Fori(2, PAIRS - 1) as i:
                for par in range(2):
                    block_work(i * 2 + par, i, par)
            one_hot_src(PICKED - 1, 1)
            fold(BLOCKS - 2, PAIRS - 1, 0)

            dve.wait_ge(s_counted, BLOCKS)
            chain(dve.tensor_copy(count[0:HI, :], p_count[0:HI, 0:LO]))
            chain(dve.tensor_tensor_scan(upto[0:HI, :], ones_lo[0:HI, :], count[0:HI, :], 0.0,
                                         ALU.mult, ALU.add))
            dve.tensor_copy(rowsum[0:HI, :], upto[0:HI, LO - 1:LO]).then_inc(s_rowsum, 1)
            chain(dve.tensor_scalar(nonempty[0:HI, :], count[0:HI, :], 0.0, None, ALU.is_gt))
            chain(dve.tensor_scalar(upto[0:HI, :], upto[0:HI, :], -1.0 - LOWEST_ROW, None, ALU.add))
            dve.wait_ge(s_poffset, 1)
            chain(dve.tensor_copy(offset[0:HI, :], p_small[0:HI, P:P + 1]))
            chain(dve.scalar_tensor_tensor(out=upto[0:HI, :], in0=upto[0:HI, :], scalar=offset[0:HI, 0:1],
                                           in1=nonempty[0:HI, :], op0=ALU.add, op1=ALU.mult))
            dve.tensor_scalar(end_idx[0:HI, :], upto[0:HI, :], float(LOWEST_ROW), None, ALU.add
                              ).then_inc(s_ends, 1)

            fold(BLOCKS - 1, PAIRS - 1, 1, tail=True)

            dve.wait_ge(s_pT, 1)
            dve.tensor_tensor_scan(carryT[:, 1:P + 1], full_capT[:, :], p_carry[:, 0:P], 0.0,
                                   ALU.min, ALU.max).then_inc(s_carryT, 1)
            dve.wait_ge(s_pcarry, 1)
            dve.wait_ge(s_fix_read, 16)
            dve.scalar_tensor_tensor(out=fixed[:, :], in0=p_carry[:, P:2 * P], scalar=caps[:, 0:1],
                                     in1=fix_rows[:, :], op0=ALU.min, op1=ALU.max).then_inc(s_fixed, 1)

            def norm_factors(g):
                l0, l1 = group_lo(g)
                dve.wait_ge(s_std, g + 1)
                chain(dve.reciprocal(rstd[0:HI, l0:l1], std[0:HI, l0:l1]))
                dve.scalar_tensor_tensor(out=shift[0:HI, l0:l1], in0=mean_var[0:HI, l0:l1, 0], scalar=-1.0,
                                         in1=rstd[0:HI, l0:l1], op0=ALU.mult, op1=ALU.mult).then_inc(s_shift, 1)

            dve.wait_ge(s_x_again, 16 * len(HI_SPLIT) * CHUNKS)
            for g in range(GROUPS):
                l0, l1 = group_lo(g)
                w = (l1 - l0) * D
                m = M[0:HI, l0:l1, :].rearrange("p l d -> p (l d)")
                xs = x_sb[0:HI, l0:l1, :].rearrange("p l d -> p (l d)")
                dve.wait_ge(s_max[g], 16 * (l1 - l0))
                dve.wait_ge(s_pA, g + 1)
                dve.tensor_tensor(m, m, p_A[g % 2][0:HI, 0:w], ALU.add).then_inc(s_sum, 1)
                if g:
                    norm_factors(g - 1)
                dve.wait_ge(s_sum, g + 1)
                dve.tensor_tensor(y[0:HI, 0:w], m, xs, ALU.add).then_inc(s_y, 1)
                dve.wait_ge(s_size, g + 1)
                dve.tensor_scalar(finite[0:HI, 0:w], size[0:HI, g % 2, 0:w], F32_MAX, None, ALU.is_lt
                                  ).then_inc(s_finite, 1)
                dve.wait_ge(s_finite, g + 1)
                dve.wait_ge(s_y, g + 1)
                chain(dve.copy_predicated(xs, finite[0:HI, 0:w], y[0:HI, 0:w]))
                for l in range(l0, l1):
                    s = dve.bn_stats(stats[0:HI, l, :], x_sb[0:HI, l, :])
                chain(s)
                for l in range(l0, l1):
                    s = dve.bn_aggr(mean_var[0:HI, l, :], stats[0:HI, l, :])
                s.then_inc(s_var, 1)
            norm_factors(GROUPS - 1)


_INS = ['x', 'src', 'dst', 'L0_gnn_W', 'L0_gnn_b']
_OUTS = [((6250, 128), 'float32')]


def kernel(**inputs):
    import numpy as np
    import concourse.bacc as bacc
    from concourse.bass_utils import run_bass_kernel_spmd

    nc = bacc.Bacc("TRN2", target_bir_lowering=False, num_devices=1)
    arrays, args = {}, []
    for name in _INS:
        a = np.ascontiguousarray(inputs[name])
        arrays[f"in_{name}_dram"] = a
        args.append(nc.dram_tensor(f"in_{name}_dram", a.shape, mybir.dt.from_np(a.dtype), kind="ExternalInput").ap())
    for i, (shape, dtype) in enumerate(_OUTS):
        args.append(nc.dram_tensor(f"out_{i}_dram", shape, mybir.dt.from_np(np.dtype(dtype)), kind="ExternalOutput").ap())
    build(nc, *args)
    r = run_bass_kernel_spmd(nc, [arrays], core_ids=[0])
    return r.results[0]["out_0_dram"]
```

```python
from contextlib import ExitStack

import concourse.bass as bass
from concourse import mybir

P = 128
F32 = mybir.dt.float32
BF16 = mybir.dt.bfloat16
I32 = mybir.dt.int32
I16 = mybir.dt.int16
ALU = mybir.AluOpType
ACT = mybir.ActivationFunctionType
AX_X = mybir.AxisListType.X

F32_MAX = 3.4028234663852886e38
ROUND = 12582912.0
EPS = 1e-5


def largest_divisor(n, most):
    return max(d for d in range(1, most + 1) if n % d == 0)


def build(nc, x, src, dst, W, b, out):
    N, D = x.shape
    E, = src.shape
    HI = largest_divisor(N, P - 1)
    LO = N // HI
    EDGE_COLS = -(-E // (2 * P)) * 2
    U = 10
    PAIRS = -(-EDGE_COLS // (2 * U))
    BLOCKS = 2 * PAIRS
    LAST_U = (EDGE_COLS - (BLOCKS - 2) * U) // 2
    GU = U - 1
    LAST_COLS = E - (P - 1) * EDGE_COLS
    PICKED = BLOCKS - 2
    PART = 3
    PARTS = GU // PART
    assert PARTS * PART == GU and LAST_U >= 2 and 0 < LAST_COLS <= EDGE_COLS and D == P
    HISTORY_ROWS = P * EDGE_COLS
    LOWEST_ROW = HISTORY_ROWS
    SPARE_ROW = HISTORY_ROWS + 1
    GROUP = 4
    GROUPS = -(-LO // GROUP)
    CHUNK_GROUPS = [0, 2, 5, 8, 11, GROUPS]
    CHUNKS = len(CHUNK_GROUPS) - 1
    AHEAD = 4
    CHUNK_LO = [min(g * GROUP, LO) for g in CHUNK_GROUPS]
    HOTS = largest_divisor(LO, U)
    HOT_LO = LO // HOTS
    HALF = P // 2
    WARM_UP = 36
    HI_SPLIT = [(0, HI // 16 * 16), (HI // 16 * 16, HI)]
    EDGE_SPLIT = [(0, 112), (112, P - 1)]
    DST_LOADS = len(EDGE_SPLIT) + 4
    SRC_LOADS = len(EDGE_SPLIT) + 1

    table = nc.dram_tensor("table", [N, D], F32, kind="Internal").ap()
    history = nc.dram_tensor("history", [SPARE_ROW + P, D], F32, kind="Internal").ap()
    history_cols = history[0:HISTORY_ROWS, :].rearrange("(p k) d -> p (k d)", p=P)
    x_rows = x.rearrange("(h l) d -> h (l d)", l=LO)
    table_rows = table.rearrange("(h l) d -> h (l d)", l=LO)
    out_rows = out.rearrange("(h l) d -> h (l d)", l=LO)

    with ExitStack() as ctx:
        def sb(name, shape, dt=F32):
            return ctx.enter_context(nc.sbuf_tensor(name, shape, dt))

        def ps(name, shape):
            return ctx.enter_context(nc.psum_tensor(name, shape, F32))

        def sem(name):
            return ctx.enter_context(nc.semaphore(name))

        x_sb = sb("x_sb", [P, LO, D])
        parts01 = x_sb[:, :, :].rearrange("p l d -> p (l d)").bitcast(BF16).rearrange(
            "p (s l d) -> p s l d", s=2, d=D)
        part2 = sb("part2", [P, LO, D], BF16)
        parts = [parts01[:, 0], parts01[:, 1], part2[:, :, :]]
        xT = sb("xT", [P, LO, HI])
        M = sb("M", [P, LO, D])
        w_sb = sb("w_sb", [P, 2 * D])
        w_diff = sb("w_diff", [P, D])
        w2T = sb("w2T", [P, D])
        wdT = sb("wdT", [P, D])
        b_row = sb("b_row", [1, GROUP * D])
        one_row = sb("one_row", [1, P])
        lowest = sb("lowest", [1, D])
        ident = sb("ident", [P, P])
        before = sb("before", [P, P])
        digit_i = sb("digit_i", [P, P], I32)
        digit = sb("digit", [P, P], BF16)
        zeros = sb("zeros", [P, P], BF16)
        eps = sb("eps", [P, 1])
        node_i = sb("node_i", [P, LO], I32)
        node = sb("node", [P, LO, HALF], I16)
        src_sb = sb("src_sb", [P, EDGE_COLS], I32)
        dst_f = sb("dst_f", [P, EDGE_COLS + 2])
        dst_i = dst_f[:, :].bitcast(I32)
        rise = sb("rise", [P, EDGE_COLS + 1])
        cap = sb("cap", [P, EDGE_COLS])
        work = sb("work", [P, EDGE_COLS])
        hi_bf = sb("hi_bf", [P, EDGE_COLS], BF16)
        lo_bf = sb("lo_bf", [P, EDGE_COLS], BF16)
        stage = [sb(f"stage{i}", [P, U], I32) for i in range(2)]
        rows = [sb(f"rows{i}", [P, U, D]) for i in range(2)]
        running = [sb(f"running{i}", [P, U, D]) for i in range(2)]
        hot_hi = [sb(f"hot_hi{i}", [P, U, HI], BF16) for i in range(2)]
        hot_lo = [sb(f"hot_lo{i}", [P, U, LO], BF16) for i in range(2)]
        src_wide = sb("src_wide", [P, P])
        src_row = [sb(f"src_row{i}", [P, P], I16) for i in range(2)]
        hot_src = sb("hot_src", [P, 2, LO, P], BF16)
        slow_B = M[:, :, :].rearrange("p l d -> p (l d)")[:, 0:N]
        slow_max = hot_src[:, :, :, :].rearrange("p s l e -> p (s l e)").bitcast(F32)[:, 0:N]
        SLOW_HI = [(h, min(h + 512 // LO, HI)) for h in range(0, HI, 512 // LO)]
        size = rows[0][:, 0:2 * GROUP, :].rearrange("p (s u) d -> p s (u d)", s=2)
        finite = rows[1][:, :, :].rearrange("p u d -> p (u d)").bitcast(I32)
        y = running[0][:, :, :].rearrange("p u d -> p (u d)")
        count = sb("count", [P, LO])
        upto = sb("upto", [P, LO])
        rowsum = sb("rowsum", [P, 1])
        offset = sb("offset", [P, 1])
        end_idx = sb("end_idx", [P, LO], I32)
        nonempty = sb("nonempty", [P, LO])
        ones_lo = sb("ones_lo", [P, LO])
        caps = sb("caps", [P, 2])
        full_bc = sb("full_bc", [P, P])
        full_capT = sb("full_capT", [P, P])
        past_first = sb("past_first", [P, 1])
        first_run = sb("first_run", [P, 1])
        has_end = sb("has_end", [P, 1])
        falls = sb("falls", [P, 1])
        ones_col = sb("ones_col", [P, 1])
        unsorted_i = sb("unsorted_i", [1, 1], I32)
        base_i = sb("base_i", [P, 2], I32)
        base_f = sb("base_f", [P, 2])
        fix_from = sb("fix_from", [P, 1])
        fix_to = sb("fix_to", [P, 1])
        fix_from_i = sb("fix_from_i", [P, 1], I32)
        fix_to_i = sb("fix_to_i", [P, 1], I32)
        fix_rows = sb("fix_rows", [P, D])
        fixed = sb("fixed", [P, D])
        carryT = sb("carryT", [P, P + 1])
        stats = sb("stats", [P, LO, 6])
        mean_var = sb("mean_var", [P, LO, 2])
        std = sb("std", [P, LO])
        rstd = sb("rstd", [P, LO])
        shift = sb("shift", [P, LO])

        p_xT = [ps(f"p_xT{i}", [P, 512]) for i in range(2)]
        p_picked = p_xT
        p_B = [ps(f"p_B{i}", [P, 512]) for i in range(2)]
        p_A = p_B
        p_w = ps("p_w", [P, 512])
        p_src = p_w
        p_order = p_w
        p_count = ps("p_count", [P, 512])
        p_small = ps("p_small", [P, 512])
        p_carry = ps("p_carry", [P, 512])

        s_const = sem("s_const")
        s_x = [sem(f"s_x{c}") for c in range(CHUNKS)]
        s_x_again = [sem(f"s_x_again{c}") for c in range(CHUNKS)]
        s_w = sem("s_w")
        s_edges_clear = sem("s_edges_clear")
        s_dst_in = sem("s_dst_in")
        s_src_in = sem("s_src_in")
        s_node_i = sem("s_node_i")
        s_node = sem("s_node")
        s_dst = sem("s_dst")
        s_rise = sem("s_rise")
        s_past_first = sem("s_past_first")
        s_cap = sem("s_cap")
        s_runs = sem("s_runs")
        s_zeros = sem("s_zeros")
        s_wdiff = sem("s_wdiff")
        s_porder = sem("s_porder")
        s_unsorted = sem("s_unsorted")
        s_slow_pB = sem("s_slow_pB")
        s_slow_B = sem("s_slow_B")
        s_slow_edges = sem("s_slow_edges")
        s_slow_turned = sem("s_slow_turned")
        s_slow_rows = sem("s_slow_rows")
        s_slow_out = sem("s_slow_out")
        s_pw = sem("s_pw")
        s_wT = sem("s_wT")
        s_pxT = sem("s_pxT")
        s_xT = sem("s_xT")
        s_pB = sem("s_pB")
        s_B = sem("s_B")
        s_part = [sem(f"s_part{i}") for i in range(3)]
        s_hi = sem("s_hi")
        s_hi_bf = sem("s_hi_bf")
        s_rest = sem("s_rest")
        s_pA = sem("s_pA")
        s_table = [sem(f"s_table{c}") for c in range(CHUNKS)]
        s_dve = sem("s_dve")
        s_lowest = sem("s_lowest")
        s_lowest_out = sem("s_lowest_out")
        s_fullbc = sem("s_fullbc")
        s_pfull = sem("s_pfull")
        s_staged = sem("s_staged")
        s_go = sem("s_go")
        s_rows = [[sem(f"s_rows{i}_{k}") for k in range(PARTS)] for i in range(2)]
        s_steps = sem("s_steps")
        s_hot = sem("s_hot")
        s_counted = sem("s_counted")
        s_wide = sem("s_wide")
        s_psrc = sem("s_psrc")
        s_src_row = sem("s_src_row")
        s_hot_src = sem("s_hot_src")
        s_picked = sem("s_picked")
        s_history = [sem(f"s_history{i}") for i in range(2)]
        s_rowsum = sem("s_rowsum")
        s_poffset = sem("s_poffset")
        s_ends = sem("s_ends")
        s_fix_read = sem("s_fix_read")
        s_pT = sem("s_pT")
        s_carryT = sem("s_carryT")
        s_pcarry = sem("s_pcarry")
        s_fixed = sem("s_fixed")
        s_fix_written = sem("s_fix_written")
        s_max = [sem(f"s_max{g}") for g in range(GROUPS)]
        s_sum = sem("s_sum")
        s_y = sem("s_y")
        s_size = sem("s_size")
        s_finite = sem("s_finite")
        s_var = sem("s_var")
        s_std = sem("s_std")
        s_shift = sem("s_shift")
        s_normed = sem("s_normed")
        s_out = sem("s_out")

        block = ctx.enter_context(nc.Block())
        LAST = (BLOCKS - 1) % 2

        def group_lo(g):
            return g * GROUP, min((g + 1) * GROUP, LO)

        def steps_of(j):
            return LAST_U if isinstance(j, int) and j >= BLOCKS - 2 else U

        def start(j):
            return (BLOCKS - 2) * U + LAST_U if isinstance(j, int) and j == BLOCKS - 1 else j * U

        def part_landed(i, k, gathers=GU):
            return i * (16 * PART) + 16 * (min(PART, gathers - k * PART) + (k == PARTS - 1))

        def chunk_of(g):
            return max(c for c in range(CHUNKS) if CHUNK_GROUPS[c] <= g)

        @block.sync
        def _(sp):
            sp.dma_start(w_sb[:, :], W).then_inc(s_w, 16)

            def load_x(c, done):
                for h0, h1 in HI_SPLIT:
                    sp.dma_start(x_sb[h0:h1, CHUNK_LO[c]:CHUNK_LO[c + 1], :],
                                 x_rows[h0:h1, CHUNK_LO[c] * D:CHUNK_LO[c + 1] * D]).then_inc(done, 16)

            for c in range(CHUNKS):
                load_x(c, s_x[c])
            sp.wait_ge(s_edges_clear, 3)
            dst_main = dst[0:(P - 1) * EDGE_COLS].rearrange("(p k) -> p k", k=EDGE_COLS)
            dst_next = dst[EDGE_COLS:EDGE_COLS * P - EDGE_COLS].rearrange("(p k) -> p k", k=EDGE_COLS)
            for p0, p1 in EDGE_SPLIT:
                sp.dma_start(dst_i[p0:p1, 1:EDGE_COLS + 1], dst_main[p0:p1, :]).then_inc(s_dst_in, 16)
            sp.dma_start(dst_i[P - 1:P, 1:LAST_COLS + 1],
                         dst[(P - 1) * EDGE_COLS:E].rearrange("(a k) -> a k", a=1)).then_inc(s_dst_in, 16)
            sp.dma_start(dst_i[1:P, 0:1], dst_main[0:P - 1, EDGE_COLS - 1:EDGE_COLS],
                         allow_slow_non_contiguous=True).then_inc(s_dst_in, 16)
            sp.dma_start(dst_i[0:P - 2, EDGE_COLS + 1:EDGE_COLS + 2], dst_next[:, 0:1],
                         allow_slow_non_contiguous=True).then_inc(s_dst_in, 16)
            sp.dma_start(dst_i[P - 2:P - 1, EDGE_COLS + 1:EDGE_COLS + 2],
                         dst[(P - 1) * EDGE_COLS:(P - 1) * EDGE_COLS + 1].rearrange("(a k) -> a k", a=1)
                         ).then_inc(s_dst_in, 16)
            src_main = src[0:(P - 1) * EDGE_COLS].rearrange("(p k) -> p k", k=EDGE_COLS)
            for p0, p1 in EDGE_SPLIT:
                sp.dma_start(src_sb[p0:p1, :], src_main[p0:p1, :]).then_inc(s_src_in, 16)
            sp.dma_start(src_sb[P - 1:P, 0:LAST_COLS],
                         src[(P - 1) * EDGE_COLS:E].rearrange("(a k) -> a k", a=1)).then_inc(s_src_in, 16)

            for c in range(CHUNKS):
                sp.wait_ge(s_B, CHUNK_GROUPS[c + 1])
                for h0, h1 in HI_SPLIT:
                    sp.dma_start(table_rows[h0:h1, CHUNK_LO[c] * D:CHUNK_LO[c + 1] * D],
                                 M[h0:h1, CHUNK_LO[c]:CHUNK_LO[c + 1], :]).then_inc(s_table[c], 16)
            for k in range(GROUP):
                sp.dma_start(b_row[0:1, k * D:(k + 1) * D], b.rearrange("(a d) -> a d", a=1)).then_inc(s_w, 16)
            sp.wait_ge(s_lowest, 1)
            sp.dma_start(history[LOWEST_ROW:LOWEST_ROW + 1, :], lowest[0:1, :]).then_inc(s_lowest_out, 16)

            def write_history(j, par, u0, u1):
                sp.wait_ge(s_steps, start(j) + u1)
                sp.dma_start(history_cols[:, bass.ds(start(j) * D + u0 * D, (u1 - u0) * D)],
                             running[par][:, u0:u1, :].rearrange("p u d -> p (u d)")
                             ).then_inc(s_history[par], 16)

            with sp.Fori(0, PAIRS - 1) as i:
                for par in range(2):
                    write_history(i * 2 + par, par, 0, U)
            write_history(BLOCKS - 2, 0, 0, LAST_U)
            for u in range(0, LAST_U, PART):
                write_history(BLOCKS - 1, 1, u, min(u + PART, LAST_U))
            sp.wait_ge(s_picked, PICKED)
            load_x(0, s_x_again[0])
            sp.wait_ge(s_max[0], 16 * GROUP)
            load_x(1, s_x_again[1])

            for g in range(GROUPS):
                l0, l1 = group_lo(g)
                sp.wait_ge(s_normed, l1)
                for h0, h1 in HI_SPLIT:
                    sp.dma_start(out_rows[h0:h1, l0 * D:l1 * D], M[h0:h1, l0:l1, :]).then_inc(s_out, 16)
                for c in range(2, CHUNKS):
                    if CHUNK_GROUPS[c] == g + AHEAD:
                        load_x(c, s_x_again[c])
            sp.wait_ge(s_out, 16 * len(HI_SPLIT) * GROUPS)

        @block.gpsimd
        def _(pool):
            pool.memset(ident[:, :], 0.0).then_inc(s_const, 1)
            pool.memset(before[:, :], 0.0).then_inc(s_const, 1)
            pool.memset(dst_i[:, LAST_COLS + 1:EDGE_COLS + 2], N).then_inc(s_edges_clear, 1)
            pool.memset(dst_i[:, 0:1], -1).then_inc(s_edges_clear, 1)
            pool.memset(src_sb[:, LAST_COLS:EDGE_COLS], 0).then_inc(s_edges_clear, 1)
            pool.wait_ge(s_const, 2)
            pool.affine_select(out=ident[:, :], in_=ident[:, :], compare_op=ALU.not_equal, fill=1.0,
                               base=0, pattern=[[-1, P]], channel_multiplier=1).then_inc(s_const, 1)
            pool.affine_select(out=before[:, :], in_=before[:, :], compare_op=ALU.is_ge, fill=1.0,
                               base=0, pattern=[[-1, P]], channel_multiplier=1).then_inc(s_const, 1)
            pool.iota(digit_i[:, :], pattern=[[1, P]], base=0, channel_multiplier=0).then_inc(s_const, 1)
            pool.iota(base_i[:, 0:1], pattern=[[0, 1]], base=0, channel_multiplier=EDGE_COLS).then_inc(s_const, 1)
            pool.iota(base_i[:, 1:2], pattern=[[0, 1]], base=SPARE_ROW, channel_multiplier=1
                      ).then_inc(s_const, 1)
            pool.iota(node_i[:, :], pattern=[[1, LO]], base=0, channel_multiplier=LO).then_inc(s_node_i, 1)
            pool.wait_ge(s_node_i, 1)
            pool.tensor_copy(node[:, :, :], node_i[:, :].unsqueeze(2).to_broadcast([P, LO, HALF])
                             ).then_inc(s_node, 1)
            pool.wait_ge(s_dst, 1)
            pool.tensor_tensor(rise[:, :], dst_f[:, 1:EDGE_COLS + 2], dst_f[:, 0:EDGE_COLS + 1],
                               ALU.subtract).then_inc(s_rise, 1)

            for c in range(CHUNKS):
                pool.wait_ge(s_table[c], 16 * len(HI_SPLIT))

            def gather_row(par, u):
                pool.indirect_dma_start(
                    out=rows[par][:, u, :], out_offset=None, in_=table[:, :],
                    in_offset=bass.IndirectOffsetOnAxis(ap=stage[par][:, u:u + 1], axis=0),
                ).then_inc(s_rows[par][min(u // PART, PARTS - 1)], 16)

            def clear_to_gather(j):
                pool.wait_ge(s_staged, j + 1)
                pool.wait_ge(s_steps, (j - 1) * U)
                pool.sem_inc(s_go, 1)

            for par in range(2):
                pool.wait_ge(s_staged, par + 1)
                for u in range(U):
                    gather_row(par, u)
            with pool.Fori(1, PAIRS - 1) as i:
                for par in range(2):
                    clear_to_gather(i * 2 + par)
                    for u in range(GU):
                        gather_row(par, u)
            for par in range(2):
                clear_to_gather(BLOCKS - 2 + par)
                for u in range(LAST_U - 1):
                    gather_row(par, u)

            last_pieces = -(-LAST_U // PART)
            pool.wait_ge(s_history[0], 16 * PAIRS)
            pool.wait_ge(s_history[1], 16 * (PAIRS - 1 + last_pieces))
            pool.wait_ge(s_lowest_out, 16)
            pool.indirect_dma_start(
                out=fix_rows[:, :], out_offset=None, in_=history[0:HISTORY_ROWS, :],
                in_offset=bass.IndirectOffsetOnAxis(ap=fix_from_i[:, 0:1], axis=0)).then_inc(s_fix_read, 16)
            pool.wait_ge(s_fixed, 1)
            pool.indirect_dma_start(
                out=history[:, :], out_offset=bass.IndirectOffsetOnAxis(ap=fix_to_i[:, 0:1], axis=0),
                in_=fixed[:, :], in_offset=None).then_inc(s_fix_written, 16)
            pool.wait_ge(s_fix_written, 16)
            pool.wait_ge(s_ends, 1)

            pool.wait_ge(s_unsorted, 1)
            unsorted = pool.value_load(unsorted_i[0:1, 0:1], min_val=0, max_val=1)
            with pool.If(unsorted > 0):
                pool.wait_ge(s_slow_rows, GROUPS + 1)
                for h0, h1 in HI_SPLIT:
                    pool.dma_start(history[0:N, :].rearrange("(h l) d -> h (l d)", l=LO)[h0:h1, :],
                                   M[h0:h1, :, :].rearrange("p l d -> p (l d)")).then_inc(s_slow_out, 16)
                pool.wait_ge(s_slow_out, 16 * len(HI_SPLIT))

            for g in range(GROUPS):
                l0, l1 = group_lo(g)
                for l in range(l0, l1):
                    pool.indirect_dma_start(
                        out=M[:, l, :], out_offset=None, in_=history[0:LOWEST_ROW + 1, :],
                        in_offset=bass.IndirectOffsetOnAxis(ap=end_idx[:, l:l + 1], axis=0),
                    ).then_inc(s_max[g], 16)

        @block.scalar
        def _(act):
            for g in range(GROUPS):
                if g == GROUPS // 2:
                    act.wait_ge(s_dst_in, 16 * DST_LOADS)
                    act.copy(dst_f[:, :], dst_i[:, :]).then_inc(s_dst, 1)
                l0, l1 = group_lo(g)
                act.wait_ge(s_pB, g + 1)
                act.copy(M[0:HI, l0:l1, :].rearrange("p l d -> p (l d)"),
                         p_B[g % 2][0:HI, 0:(l1 - l0) * D]).then_inc(s_B, 1)

            def stage_block(j, i, par):
                if not (isinstance(j, int) and j < 2):
                    for k in range(PARTS):
                        act.wait_ge(s_rows[par][k], part_landed(i - 1, k))
                act.copy(stage[par][:, 0:steps_of(j)], src_sb[:, bass.ds(start(j), steps_of(j))]
                         ).then_inc(s_staged, 1)

            def src_to_row(q, par):
                if isinstance(q, int):
                    last = start(q + 2) + steps_of(q + 2) - 1
                else:
                    last = q * U + (2 * U + U - 1)
                if not (isinstance(q, int) and q == 0):
                    act.wait_ge(s_psrc, q)
                act.copy(src_wide[:, :], src_sb[:, bass.ds(last, 1)].to_broadcast([P, P])
                         ).then_inc(s_wide, 1)
                act.wait_ge(s_psrc, q + 1)
                if not (isinstance(q, int) and q < 2):
                    act.wait_ge(s_hot_src, (q - 1) * HOTS)
                act.copy(src_row[par][:, :], p_src[:, 0:P]).then_inc(s_src_row, 1)

            act.wait_ge(s_src_in, 16 * SRC_LOADS)
            for par in range(2):
                stage_block(par, 0, par)

            act.wait_ge(s_pxT, GROUPS)
            act.wait_ge(s_B, GROUPS)
            for n in range(2):
                for c in range(CHUNKS):
                    l0, l1 = CHUNK_LO[c], CHUNK_LO[c + 1]
                    if n:
                        act.wait_ge(s_rest, c + 1)
                    act.copy(parts[n][0:HI, l0:l1, :], M[0:HI, l0:l1, :]).then_inc(s_part[n], 1)
                src_to_row(n, n)
            act.wait_ge(s_hi, 1)
            act.copy(hi_bf[:, :], work[:, :]).then_inc(s_hi_bf, 1)

            act.wait_ge(s_cap, 1)
            act.activation(rise[:, :], rise[:, :], ACT.Relu, scale=-1.0, accum_out=falls[:, 0:1]
                           ).then_inc(s_runs, 1)
            act.wait_ge(s_past_first, 1)
            act.wait_ge(s_runs, 1)
            act.activation(rise[:, 0:EDGE_COLS], dst_f[:, 1:EDGE_COLS + 1], ACT.Relu, scale=-1.0,
                           bias=past_first[:, 0:1], accum_out=first_run[:, 0:1]).then_inc(s_runs, 1)
            for q in range(2, 4):
                stage_block(q, 1, q % 2)
                src_to_row(q, q % 2)
            with act.Fori(2, PAIRS - 2) as i:
                for par in range(2):
                    stage_block(i * 2 + par, i, par)
                    src_to_row(i * 2 + par, par)
            for par in range(2):
                stage_block(BLOCKS - 4 + par, PAIRS - 2, par)
                src_to_row(BLOCKS - 4 + par, par)
            for par in range(2):
                stage_block(BLOCKS - 2 + par, PAIRS - 1, par)

            def scale_and_shift(g):
                l0, l1 = group_lo(g)
                act.wait_ge(s_shift, g + 1)
                for l in range(l0, l1):
                    act.activation(M[0:HI, l, :], x_sb[0:HI, l, :], ACT.Identity,
                                   scale=rstd[0:HI, l:l + 1], bias=shift[0:HI, l:l + 1]).then_inc(s_normed, 1)

            for g in range(GROUPS):
                l0, l1 = group_lo(g)
                w = (l1 - l0) * D
                act.wait_ge(s_sum, g + 1)
                if g >= 2:
                    act.wait_ge(s_finite, g - 1)
                act.activation(size[0:HI, g % 2, 0:w], M[0:HI, l0:l1, :].rearrange("p l d -> p (l d)"),
                               ACT.Abs).then_inc(s_size, 1)
                if g:
                    scale_and_shift(g - 1)
                act.wait_ge(s_var, g + 1)
                act.activation(std[0:HI, l0:l1], mean_var[0:HI, l0:l1, 1], ACT.Sqrt,
                               bias=eps[0:HI, 0:1]).then_inc(s_std, 1)
            scale_and_shift(GROUPS - 1)

        @block.tensor
        def _(pe):
            pe.wait_ge(s_zeros, 1)
            for _ in range(WARM_UP):
                pe.matmul(p_count[:, 0:P], zeros[:, :], zeros[:, :], start=True, stop=True)
            pe.wait_ge(s_const, 4)
            pe.wait_ge(s_wdiff, 1)
            pe.transpose(p_w[:, 0:D], w_sb[:, D:2 * D], ident[:, :]).then_inc(s_pw, 1)
            pe.transpose(p_w[:, D:2 * D], w_diff[:, :], ident[:, :]).then_inc(s_pw, 1)

            def transpose_x(g):
                l0, l1 = group_lo(g)
                pe.wait_ge(s_x[chunk_of(g)], 16 * len(HI_SPLIT))
                if g >= 2:
                    pe.wait_ge(s_xT, g - 1)
                for l in range(l0, l1):
                    mm = pe.transpose(p_xT[g % 2][:, (l - l0) * HI:(l - l0 + 1) * HI],
                                      x_sb[0:HI, l, :], ident[0:HI, 0:HI])
                mm.then_inc(s_pxT, 1)

            def project_B(g):
                l0, l1 = group_lo(g)
                pe.wait_ge(s_xT, g + 1)
                if g == 0:
                    pe.wait_ge(s_wT, 2)
                if g >= 2:
                    pe.wait_ge(s_B, g - 1)
                for l in range(l0, l1):
                    mm = pe.matmul(p_B[g % 2][0:HI, (l - l0) * D:(l - l0 + 1) * D], xT[:, l, :], w2T[:, :],
                                   start=True, stop=True)
                mm.then_inc(s_pB, 1)

            transpose_x(0)
            for g in range(GROUPS):
                if g + 1 < GROUPS:
                    transpose_x(g + 1)
                project_B(g)

            def turn_src(q):
                pe.wait_ge(s_wide, q + 1)
                if not (isinstance(q, int) and q == 0):
                    pe.wait_ge(s_src_row, q)
                pe.transpose(p_src[:, 0:P], src_wide[:, :], ident[:, :]).then_inc(s_psrc, 1)

            def pick_rows(q, par):
                if not (isinstance(q, int) and q < 2):
                    pe.wait_ge(s_steps, (q + 1) * U)
                for l in range(LO):
                    if l % HOT_LO == 0:
                        pe.wait_ge(s_hot_src, q * HOTS + (l // HOT_LO + 1))
                    for n in range(3):
                        mm = pe.matmul(p_picked[par][:, 0:D], hot_src[0:HI, par, l, :], parts[n][0:HI, l, :],
                                       start=(l == 0 and n == 0), stop=(l == LO - 1 and n == 2))
                mm.then_inc(s_picked, 1)

            def count_block(j, par):
                pe.wait_ge(s_hot, j * 2 + 2)
                for u in range(steps_of(j)):
                    mm = pe.matmul(p_count[0:HI, 0:LO], hot_hi[par][:, u, :], hot_lo[par][:, u, :],
                                   start=False, stop=False, skip_group_check=True)
                mm.then_inc(s_counted, 1)

            pe.matmul(p_count[0:HI, 0:LO], zeros[:, 0:HI], zeros[:, 0:LO], start=True, stop=False,
                      skip_group_check=True)
            turn_src(0)
            turn_src(1)
            pe.wait_ge(s_part[2], CHUNKS)

            def picks_and_counts(j, par, turn=True):
                if turn:
                    turn_src(j + 2)
                pick_rows(j, par)
                count_block(j, par)

            for j in range(2):
                turn_src(j + 2)
                pick_rows(j, j)
            for j in range(2):
                count_block(j, j)
            with pe.Fori(1, PAIRS - 2) as i:
                for par in range(2):
                    picks_and_counts(i * 2 + par, par)
            for j in range(BLOCKS - 4, BLOCKS - 2):
                picks_and_counts(j, j % 2, turn=False)
            pe.wait_ge(s_fullbc, 1)
            pe.transpose(p_small[:, 0:P], full_bc[:, :], ident[:, :]).then_inc(s_pfull, 1)
            count_block(BLOCKS - 2, 0)

            pe.wait_ge(s_steps, EDGE_COLS)
            pe.transpose(p_carry[:, 0:P], running[LAST][:, LAST_U - 1, :], ident[:, :]).then_inc(s_pT, 1)
            pe.wait_ge(s_runs, 1)
            pe.matmul(p_order[0:1, 0:1], falls[:, 0:1], ones_col[:, 0:1],
                      start=True, stop=True).then_inc(s_porder, 1)
            pe.wait_ge(s_carryT, 1)
            pe.transpose(p_carry[:, P:2 * P], carryT[:, 0:P], ident[:, :]).then_inc(s_pcarry, 1)
            count_block(BLOCKS - 1, 1)
            pe.wait_ge(s_rowsum, 1)
            pe.matmul(p_small[0:HI, P:P + 1], before[0:HI, 0:HI], rowsum[0:HI, 0:1],
                      start=True, stop=True).then_inc(s_poffset, 1)

            pe.wait_ge(s_unsorted, 1)
            unsorted = pe.value_load(unsorted_i[0:1, 0:1], min_val=0, max_val=1)
            with pe.If(unsorted > 0):
                for c, (h0, h1) in enumerate(SLOW_HI):
                    if c >= 2:
                        pe.wait_ge(s_slow_B, c - 1)
                    pe.matmul(p_B[c % 2][:, 0:(h1 - h0) * LO], w2T[:, :],
                              xT[:, :, h0:h1].rearrange("c l h -> c h l"),
                              start=True, stop=True).then_inc(s_slow_pB, 1)
                pe.wait_ge(s_slow_edges, 1)
                for g in range(GROUPS):
                    l0, l1 = group_lo(g)
                    if g >= 2:
                        pe.wait_ge(s_slow_rows, g - 1)
                    for l in range(l0, l1):
                        mm = pe.transpose(p_B[g % 2][0:HI, (l - l0) * D:(l - l0 + 1) * D],
                                          slow_max[:, :].rearrange("p (h l) -> p h l", l=LO)[:, :, l],
                                          ident[:, :])
                    mm.then_inc(s_slow_turned, 1)
                pe.wait_ge(s_slow_rows, GROUPS)

            pe.wait_ge(s_w, 16 * (1 + GROUP))
            for g in range(GROUPS):
                l0, l1 = group_lo(g)
                if g >= 2:
                    pe.wait_ge(s_sum, g - 1)
                pe.matmul(p_A[g % 2][0:HI, 0:(l1 - l0) * D], one_row[0:1, 0:HI], b_row[0:1, 0:(l1 - l0) * D],
                          start=True, stop=False, skip_group_check=True)
                for l in range(l0, l1):
                    mm = pe.matmul(p_A[g % 2][0:HI, (l - l0) * D:(l - l0 + 1) * D], xT[:, l, :], wdT[:, :],
                                   start=False, stop=True, skip_group_check=True)
                mm.then_inc(s_pA, 1)

        @block.vector
        def _(dve):
            done = [0]

            def chain(ins):
                done[0] += 1
                ins.then_inc(s_dve, 1)
                dve.wait_ge(s_dve, done[0])

            dve.memset(zeros[:, :], 0.0).then_inc(s_zeros, 1)
            dve.memset(lowest[:, :], -F32_MAX).then_inc(s_lowest, 1)
            dve.memset(eps[:, :], EPS)
            dve.memset(ones_lo[:, :], 1.0)
            dve.memset(ones_col[:, :], 1.0)
            dve.memset(one_row[:, :], 1.0)
            dve.memset(end_idx[:, :], 0)
            dve.memset(carryT[:, 0:1], 0.0)
            chain(dve.memset(running[1][:, U - 1, :], 0.0))
            dve.wait_ge(s_w, 16)
            dve.tensor_tensor(w_diff[:, :], w_sb[:, 0:D], w_sb[:, D:2 * D], ALU.subtract).then_inc(s_wdiff, 1)
            dve.wait_ge(s_pw, 2)
            dve.tensor_copy(w2T[:, :], p_w[:, 0:D]).then_inc(s_wT, 1)
            dve.tensor_copy(wdT[:, :], p_w[:, D:2 * D]).then_inc(s_wT, 1)

            for g in range(GROUPS):
                l0, l1 = group_lo(g)
                dve.wait_ge(s_pxT, g + 1)
                dve.tensor_copy(xT[:, l0:l1, :].rearrange("p l h -> p (l h)"),
                                p_xT[g % 2][:, 0:(l1 - l0) * HI]).then_inc(s_xT, 1)

            dve.wait_ge(s_dst, 1)
            dve.wait_ge(s_const, 7)
            dve.tensor_scalar(past_first[:, :], dst_f[:, 1:2], 1.0, None, ALU.add).then_inc(s_past_first, 1)
            dve.wait_ge(s_rise, 1)
            dve.tensor_scalar(cap[:, :], rise[:, 0:EDGE_COLS], 0.0, 0.5, ALU.is_equal, ALU.subtract
                              ).then_inc(s_cap, 1)
            dve.wait_ge(s_cap, 1)
            chain(dve.tensor_scalar(cap[:, :], cap[:, :], F32_MAX, 2.0, ALU.mult, ALU.mult))
            chain(dve.memset(cap[:, 0:1], -F32_MAX))

            def subtract_part(n):
                for c in range(CHUNKS):
                    l0, l1 = CHUNK_LO[c], CHUNK_LO[c + 1]
                    dve.wait_ge(s_part[n], c + 1)
                    if n == 0:
                        dve.wait_ge(s_table[c], 16 * len(HI_SPLIT))
                    rest, there = (M, s_rest) if n == 0 else (part2, s_part[2])
                    dve.tensor_tensor(rest[0:HI, l0:l1, :], M[0:HI, l0:l1, :], parts[n][0:HI, l0:l1, :],
                                      ALU.subtract).then_inc(there, 1)

            def one_hot_src(q, par, h):
                if h == 0:
                    dve.wait_ge(s_src_row, q + 1)
                    if not (isinstance(q, int) and q < 2):
                        dve.wait_ge(s_picked, q - 1)
                row = src_row[par][:, :].rearrange("p (a e) -> p a e", e=HALF)
                l0 = h * HOT_LO
                dve.tensor_tensor(
                    hot_src[:, par, l0:l0 + HOT_LO, :].rearrange("p l (a e) -> p l a e", e=HALF),
                    row.unsqueeze(1).to_broadcast([P, HOT_LO, 2, HALF]),
                    node[:, l0:l0 + HOT_LO, :].unsqueeze(2).to_broadcast([P, HOT_LO, 2, HALF]),
                    ALU.is_equal).then_inc(s_hot_src, 1)

            def one_hots_dst(j, par):
                if not (isinstance(j, int) and j < 2):
                    dve.wait_ge(s_counted, j - 1)
                for hot, dig, width in ((hot_hi, hi_bf, HI), (hot_lo, lo_bf, LO)):
                    n = steps_of(j)
                    dve.tensor_tensor(hot[par][:, 0:n, :],
                                      dig[:, bass.ds(start(j), n)].unsqueeze(2).to_broadcast([P, n, width]),
                                      digit[:, 0:width].unsqueeze(1).to_broadcast([P, n, width]),
                                      ALU.is_equal).then_inc(s_hot, 1)

            def fold(j, i, par, hot=True):
                first = isinstance(j, int) and j < 2
                if not first:
                    dve.wait_ge(s_history[par], i * 16)
                n = steps_of(j)
                for u in range(n):
                    earlier = running[par][:, u - 1, :] if u else running[1 - par][:, steps_of(j - 1) - 1, :]
                    row = rows[par][:, u, :]
                    if u < n - 1 and u % PART == 0:
                        dve.wait_ge(s_rows[par][u // PART], part_landed(i, u // PART, n - 1))
                    if u == n - 1 and not first:
                        dve.wait_ge(s_picked, j - 1)
                        row = p_picked[par][:, 0:D]
                    if not (first and j == 0 and u == 0):
                        dve.wait_ge(s_steps, start(j) + u)
                    dve.scalar_tensor_tensor(out=running[par][:, u, :], in0=earlier,
                                             scalar=cap[:, bass.ds(start(j) + u, 1)],
                                             in1=row, op0=ALU.min, op1=ALU.max).then_inc(s_steps, 1)
                    if hot and u < HOTS:
                        one_hot_src(j, par, u)

            subtract_part(0)
            dst_own = dst_f[:, 1:EDGE_COLS + 1]
            dve.tensor_copy(digit[:, :], digit_i[:, :])
            chain(dve.tensor_scalar(work[:, :], dst_own, (LO - 1) / 2.0, 1.0 / LO, ALU.subtract, ALU.mult))
            chain(dve.tensor_scalar(work[:, :], work[:, :], ROUND, None, ALU.add))
            dve.tensor_scalar(work[:, :], work[:, :], ROUND, None, ALU.subtract).then_inc(s_hi, 1)
            subtract_part(1)
            dve.wait_ge(s_node, 1)
            fold(0, 0, 0)
            dve.wait_ge(s_hi, 1)
            chain(dve.scalar_tensor_tensor(out=lo_bf[:, :], in0=work[:, :], scalar=-float(LO), in1=dst_own,
                                           op0=ALU.mult, op1=ALU.add))
            fold(1, 0, 1)
            dve.wait_ge(s_hi_bf, 1)
            for j in range(2):
                one_hots_dst(j, j)
            with dve.Fori(1, PAIRS - 1) as i:
                for par in range(2):
                    fold(i * 2 + par, i, par)
                    one_hots_dst(i * 2 + par, par)

            for k, (first, last) in enumerate(((0, 1), (0, EDGE_COLS))):
                dve.tensor_tensor(caps[:, k:k + 1], dst_f[:, first:first + 1], dst_f[:, last:last + 1],
                                  ALU.is_equal).then_inc(s_dve, 1)
            done[0] += 2
            dve.wait_ge(s_dve, done[0])
            chain(dve.tensor_scalar(caps[:, :], caps[:, :], 0.5, F32_MAX, ALU.subtract, ALU.mult))
            chain(dve.tensor_scalar(caps[:, :], caps[:, :], 2.0, None, ALU.mult))
            dve.tensor_copy(full_bc[:, :], caps[:, 1:2].to_broadcast([P, P])).then_inc(s_fullbc, 1)
            one_hots_dst(BLOCKS - 2, 0)

            chain(dve.tensor_copy(base_f[:, :], base_i[:, :]))
            chain(dve.tensor_tensor(has_end[:, :], dst_f[:, 1:2], dst_f[:, EDGE_COLS + 1:EDGE_COLS + 2],
                                    ALU.not_equal))
            dve.wait_ge(s_runs, 2)
            chain(dve.tensor_scalar(fix_from[:, :], first_run[:, :], float(EDGE_COLS), -1.0, ALU.min, ALU.add))
            chain(dve.tensor_tensor(fix_from[:, :], fix_from[:, :], base_f[:, 0:1], ALU.add))
            chain(dve.tensor_tensor(fix_to[:, :], fix_from[:, :], base_f[:, 1:2], ALU.subtract))
            chain(dve.scalar_tensor_tensor(out=fix_to[:, :], in0=fix_to[:, :], scalar=has_end[:, 0:1],
                                           in1=base_f[:, 1:2], op0=ALU.mult, op1=ALU.add))
            dve.tensor_copy(fix_from_i[:, :], fix_from[:, :])
            chain(dve.tensor_copy(fix_to_i[:, :], fix_to[:, :]))
            fold(BLOCKS - 2, PAIRS - 1, 0, hot=False)
            fold(BLOCKS - 1, PAIRS - 1, 1, hot=False)

            dve.wait_ge(s_pfull, 1)
            chain(dve.tensor_copy(full_capT[:, :], p_small[:, 0:P]))
            dve.wait_ge(s_pT, 1)
            dve.tensor_tensor_scan(carryT[:, 1:P + 1], full_capT[:, :], p_carry[:, 0:P], 0.0,
                                   ALU.min, ALU.max).then_inc(s_carryT, 1)
            one_hots_dst(BLOCKS - 1, 1)

            dve.wait_ge(s_counted, BLOCKS)
            chain(dve.tensor_copy(count[0:HI, :], p_count[0:HI, 0:LO]))
            chain(dve.tensor_tensor_scan(upto[0:HI, :], ones_lo[0:HI, :], count[0:HI, :], 0.0,
                                         ALU.mult, ALU.add))
            dve.tensor_copy(rowsum[0:HI, :], upto[0:HI, LO - 1:LO]).then_inc(s_rowsum, 1)
            chain(dve.tensor_scalar(nonempty[0:HI, :], count[0:HI, :], 0.0, None, ALU.is_gt))
            chain(dve.tensor_scalar(upto[0:HI, :], upto[0:HI, :], -1.0 - LOWEST_ROW, None, ALU.add))
            dve.wait_ge(s_poffset, 1)
            chain(dve.tensor_copy(offset[0:HI, :], p_small[0:HI, P:P + 1]))
            chain(dve.scalar_tensor_tensor(out=upto[0:HI, :], in0=upto[0:HI, :], scalar=offset[0:HI, 0:1],
                                           in1=nonempty[0:HI, :], op0=ALU.add, op1=ALU.mult))
            dve.tensor_scalar(end_idx[0:HI, :], upto[0:HI, :], float(LOWEST_ROW), None, ALU.add
                              ).then_inc(s_ends, 1)

            dve.wait_ge(s_porder, 1)
            dve.tensor_scalar(unsorted_i[:, :], p_order[0:1, 0:1], 0.0, None, ALU.is_gt
                              ).then_inc(s_unsorted, 1)

            dve.wait_ge(s_pcarry, 1)
            dve.wait_ge(s_fix_read, 16)
            dve.scalar_tensor_tensor(out=fixed[:, :], in0=p_carry[:, P:2 * P], scalar=caps[:, 0:1],
                                     in1=fix_rows[:, :], op0=ALU.min, op1=ALU.max).then_inc(s_fixed, 1)

            dve.wait_ge(s_unsorted, 1)
            unsorted = dve.value_load(unsorted_i[0:1, 0:1], min_val=0, max_val=1)
            with dve.If(unsorted > 0):
                for c, (h0, h1) in enumerate(SLOW_HI):
                    dve.wait_ge(s_slow_pB, c + 1)
                    dve.tensor_copy(slow_B[:, h0 * LO:h1 * LO], p_B[c % 2][:, 0:(h1 - h0) * LO]
                                    ).then_inc(s_slow_B, 1)
                dve.memset(slow_max, -F32_MAX)
                dve.drain()
                with dve.Fori(0, E) as e:
                    s = dve.value_load(src[bass.ds(e, 1)].rearrange("(a k) -> a k", a=1), min_val=0, max_val=N - 1)
                    d = dve.value_load(dst[bass.ds(e, 1)].rearrange("(a k) -> a k", a=1), min_val=0, max_val=N - 1)
                    dve.tensor_tensor(slow_max[:, bass.ds(d, 1)], slow_max[:, bass.ds(d, 1)],
                                      slow_B[:, bass.ds(s, 1)], ALU.max)
                    dve.drain()
                dve.memset(falls[:, :], 0.0).then_inc(s_slow_edges, 1)
                for g in range(GROUPS):
                    l0, l1 = group_lo(g)
                    dve.wait_ge(s_slow_turned, g + 1)
                    dve.tensor_copy(M[0:HI, l0:l1, :].rearrange("p l d -> p (l d)"),
                                    p_B[g % 2][0:HI, 0:(l1 - l0) * D]).then_inc(s_slow_rows, 1)
                dve.wait_ge(s_fix_written, 16)
                dve.tensor_copy(end_idx[0:HI, :], node_i[0:HI, :]).then_inc(s_slow_rows, 1)

            def norm_factors(g):
                l0, l1 = group_lo(g)
                dve.wait_ge(s_std, g + 1)
                chain(dve.reciprocal(rstd[0:HI, l0:l1], std[0:HI, l0:l1]))
                dve.scalar_tensor_tensor(out=shift[0:HI, l0:l1], in0=mean_var[0:HI, l0:l1, 0], scalar=-1.0,
                                         in1=rstd[0:HI, l0:l1], op0=ALU.mult, op1=ALU.mult).then_inc(s_shift, 1)

            for g in range(GROUPS):
                l0, l1 = group_lo(g)
                w = (l1 - l0) * D
                m = M[0:HI, l0:l1, :].rearrange("p l d -> p (l d)")
                xs = x_sb[0:HI, l0:l1, :].rearrange("p l d -> p (l d)")
                dve.wait_ge(s_max[g], 16 * (l1 - l0))
                dve.wait_ge(s_pA, g + 1)
                dve.wait_ge(s_x_again[chunk_of(g)], 16 * len(HI_SPLIT))
                dve.tensor_tensor(m, m, p_A[g % 2][0:HI, 0:w], ALU.add).then_inc(s_sum, 1)
                if g:
                    norm_factors(g - 1)
                dve.wait_ge(s_sum, g + 1)
                dve.tensor_tensor(y[0:HI, 0:w], m, xs, ALU.add).then_inc(s_y, 1)
                dve.wait_ge(s_size, g + 1)
                dve.tensor_scalar(finite[0:HI, 0:w], size[0:HI, g % 2, 0:w], F32_MAX, None, ALU.is_lt
                                  ).then_inc(s_finite, 1)
                dve.wait_ge(s_finite, g + 1)
                dve.wait_ge(s_y, g + 1)
                chain(dve.copy_predicated(xs, finite[0:HI, 0:w], y[0:HI, 0:w]))
                for l in range(l0, l1):
                    s = dve.bn_stats(stats[0:HI, l, :], x_sb[0:HI, l, :])
                chain(s)
                for l in range(l0, l1):
                    s = dve.bn_aggr(mean_var[0:HI, l, :], stats[0:HI, l, :])
                s.then_inc(s_var, 1)
            norm_factors(GROUPS - 1)


_INS = ['x', 'src', 'dst', 'L0_gnn_W', 'L0_gnn_b']
_OUTS = [((6250, 128), 'float32')]


def kernel(**inputs):
    import numpy as np
    import concourse.bacc as bacc
    from concourse.bass_utils import run_bass_kernel_spmd

    nc = bacc.Bacc("TRN2", target_bir_lowering=False, num_devices=1)
    arrays, args = {}, []
    for name in _INS:
        a = np.ascontiguousarray(inputs[name])
        arrays[f"in_{name}_dram"] = a
        args.append(nc.dram_tensor(f"in_{name}_dram", a.shape, mybir.dt.from_np(a.dtype), kind="ExternalInput").ap())
    for i, (shape, dtype) in enumerate(_OUTS):
        args.append(nc.dram_tensor(f"out_{i}_dram", shape, mybir.dt.from_np(np.dtype(dtype)), kind="ExternalOutput").ap())
    build(nc, *args)
    r = run_bass_kernel_spmd(nc, [arrays], core_ids=[0])
    return r.results[0]["out_0_dram"]
```
